# Optimizing a Trainium2 kernel written in Bass

```python
import numpy as np
import jax
import jax.numpy as jnp

def _softmax(x, axis=-1):
    return jax.nn.softmax(x, axis=axis)

def _gelu(x):
    return jax.nn.gelu(x, approximate=True)

def _silu(x):
    return jax.nn.silu(x)

def _sigmoid(x):
    return jax.nn.sigmoid(x)

def _layernorm(x, axis=-1, eps=1e-05):
    m = jnp.mean(x, axis=axis, keepdims=True)
    v = jnp.var(x, axis=axis, keepdims=True)
    return (x - m) / jnp.sqrt(v + eps)

def _scatter_add(tgt, idx, src, axis=0):
    return tgt.at[idx].add(src)

def _segment_sum(src, seg, n):
    return jax.ops.segment_sum(src, seg, n)
kernel_name = 'mk_xattn_ffn_d2_seqx_r4_a62358'

def setup_inputs(seed: int=0):
    np.random.seed(seed)
    _w = jnp.asarray

    def _rec_inputs():
        import jax
        import jax.numpy as jnp
        _rk = jax.random.key(seed)
        x = -0.0003929 + 0.9999 * jax.random.normal(jax.random.fold_in(_rk, 1), (16, 112, 256), jnp.float32)
        _lenS = 112 - jax.random.randint(jax.random.fold_in(_rk, 7), (16,), 0, max(1, 112 // 4) + 1, jnp.int32)
        _lenS2 = 375 - jax.random.randint(jax.random.fold_in(_rk, 8), (16,), 0, max(1, 375 // 4) + 1, jnp.int32)
        _ctx_1024P = jax.random.normal(jax.random.fold_in(_rk, 11), (16, 16, 256), jnp.float32)
        _ctx_1024c = jax.random.dirichlet(jax.random.fold_in(_rk, 511), 0.3 * jnp.ones((16,), jnp.float32), (16, 375))
        _ctx_1024t = jnp.einsum('bsk,bkd->bsd', _ctx_1024c, _ctx_1024P)
        _ctx_1024t = _ctx_1024t * jax.lax.rsqrt(jnp.mean(jnp.square(_ctx_1024t)) + 1e-12) * 0.953939
        ctx_1024 = 2.81802e-05 + 1.00001 * (_ctx_1024t + 0.3 * jax.random.normal(jax.random.fold_in(_rk, 611), (16, 375, 256), jnp.float32))
        _validS = jnp.arange(112)[None, :] < _lenS[:, None]
        _validS2 = jnp.arange(375)[None, :] < _lenS2[:, None]
        _causal = jnp.tril(jnp.ones((112, 112), dtype=bool))
        mask_Bx1xS2_ik1 = jnp.where(jnp.broadcast_to(_validS2[:, None, :], (16, 1, 375)), 1, 0).astype(jnp.int32)
        return (x, ctx_1024, mask_Bx1xS2_ik1)
    x, ctx_1024, mask_Bx1xS2_ik1 = _rec_inputs()

    def _L0_xattn_setup():
        import jax, jax.numpy as jnp
        import numpy as np
        B, NQ, NK = (8, 512, 512)
        DQ = DK = DV = 256
        EPS = 1e-05

        def _xavier(key, shape):
            fan_in, fan_out = (shape[0], shape[1])
            lim = float(np.sqrt(6.0 / (fan_in + fan_out)))
            return jax.random.uniform(key, shape, jnp.float32, -lim, lim)

        def _layernorm(x, g, b):
            mu = jnp.mean(x, axis=-1, keepdims=True)
            var = jnp.mean(jnp.square(x - mu), axis=-1, keepdims=True)
            return (x - mu) * jax.lax.rsqrt(var + EPS) * g + b
        key = jax.random.key(seed)
        ks = jax.random.split(key, 12)
        return {'Q': jax.random.normal(ks[0], (B, NQ, DQ), jnp.float32), 'K': jax.random.normal(ks[1], (B, NK, DK), jnp.float32), 'V': jax.random.normal(ks[2], (B, NK, DK), jnp.float32), 'pad_mask': jax.random.randint(ks[3], (B, 1, NK), 0, 2, jnp.int32), 'Wq': _xavier(ks[4], (DQ, DV)), 'bq': jnp.zeros((DV,), jnp.float32), 'Wk': _xavier(ks[5], (DK, DV)), 'bk': jnp.zeros((DV,), jnp.float32), 'Wv': _xavier(ks[6], (DK, DV)), 'bv': jnp.zeros((DV,), jnp.float32), 'Wo': _xavier(ks[7], (DV, DV)), 'bo': jnp.zeros((DV,), jnp.float32), 'g0': jnp.ones((DV,), jnp.float32), 'beta0': jnp.zeros((DV,), jnp.float32)}
    _L0_xattn_all = _L0_xattn_setup()
    _L0_xattn_in = {k: v for k, v in _L0_xattn_all.items() if k in ('Wq', 'bq', 'Wk', 'bk', 'Wv', 'bv', 'Wo', 'bo', 'g0', 'beta0')}
    del _L0_xattn_all

    def _L0_ffn_setup():
        import jax, jax.numpy as jnp
        import numpy as np
        B, T, D, H = (4, 512, 256, 512)
        E, S, K = (8, 2, 2)

        def _swiglu_stacked(x, w1, b1, w2, b2, w3, b3):
            p1 = jnp.einsum('btd,ndh->nbth', x, w1) + b1[:, None, None, :]
            p2 = jnp.einsum('btd,ndh->nbth', x, w2) + b2[:, None, None, :]
            glu = jax.nn.silu(p1) * p2
            return jnp.einsum('nbth,nhd->nbtd', glu, w3) + b3[:, None, None, :]
        key = jax.random.key(seed)
        ks = jax.random.split(key, 10)
        s = 0.02
        return {'x': jax.random.normal(ks[0], (B, T, D), jnp.float32), 'gate_w': jax.random.normal(ks[1], (D, E), jnp.float32) * s, 'gate_b': jnp.zeros((E,), jnp.float32), 'rw1': jax.random.normal(ks[2], (E, D, H), jnp.float32) * s, 'rb1': jnp.zeros((E, H), jnp.float32), 'rw2': jax.random.normal(ks[3], (E, D, H), jnp.float32) * s, 'rb2': jnp.zeros((E, H), jnp.float32), 'rw3': jax.random.normal(ks[4], (E, H, D), jnp.float32) * s, 'rb3': jnp.zeros((E, D), jnp.float32), 'sw1': jax.random.normal(ks[5], (S, D, H), jnp.float32) * s, 'sb1': jnp.zeros((S, H), jnp.float32), 'sw2': jax.random.normal(ks[6], (S, D, H), jnp.float32) * s, 'sb2': jnp.zeros((S, H), jnp.float32), 'sw3': jax.random.normal(ks[7], (S, H, D), jnp.float32) * s, 'sb3': jnp.zeros((S, D), jnp.float32)}
    _L0_ffn_all = _L0_ffn_setup()
    _L0_ffn_in = {k: v for k, v in _L0_ffn_all.items() if k in ('gate_w', 'gate_b', 'rw1', 'rb1', 'rw2', 'rb2', 'rw3', 'rb3', 'sw1', 'sb1', 'sw2', 'sb2', 'sw3', 'sb3')}
    del _L0_ffn_all

    def _L1_xattn_setup():
        import jax, jax.numpy as jnp
        import numpy as np
        B, S, D, H = (2, 512, 256, 16)
        HD = D // H
        key = jax.random.key(seed)
        ks = jax.random.split(key, 7)
        s = 0.02
        return {'queries': jax.random.normal(ks[0], (B, S, D), jnp.float32), 'keys': jax.random.normal(ks[1], (B, S, D), jnp.float32), 'values': jax.random.normal(ks[2], (B, S, D), jnp.float32), 'Wq': jax.random.normal(ks[3], (D, D), jnp.float32) * s, 'Wk': jax.random.normal(ks[4], (D, D), jnp.float32) * s, 'Wv': jax.random.normal(ks[5], (D, D), jnp.float32) * s, 'Wo': jax.random.normal(ks[6], (D, D), jnp.float32) * s}
    _L1_xattn_all = _L1_xattn_setup()
    _L1_xattn_in = {k: v for k, v in _L1_xattn_all.items() if k in ('Wq', 'Wk', 'Wv', 'Wo')}
    del _L1_xattn_all

    def _L1_ffn_setup():
        import jax, jax.numpy as jnp
        import numpy as np
        key = jax.random.key(seed)
        k1, k2, k3, k4, k5 = jax.random.split(key, 5)
        d_in, d_out, r = (256, 256, 32)
        x = jax.random.normal(k1, (8, 2048, d_in), dtype=jnp.float32)
        W = jax.random.normal(k2, (d_out, d_in), dtype=jnp.float32) * (1.0 / np.sqrt(d_in))
        b = jax.random.normal(k3, (d_out,), dtype=jnp.float32) * 0.01
        V_r = jax.random.normal(k4, (d_in, r), dtype=jnp.float32) * (1.0 / np.sqrt(d_in))
        C = jax.random.normal(k5, (d_out, r), dtype=jnp.float32) * (1.0 / np.sqrt(r))
        return {'x': x, 'W': W, 'b': b, 'V_r': V_r, 'C': C}
    _L1_ffn_all = _L1_ffn_setup()
    _L1_ffn_in = {k: v for k, v in _L1_ffn_all.items() if k in ('W', 'b', 'V_r', 'C')}
    del _L1_ffn_all
    return {'x': x, 'ctx_1024': ctx_1024, 'mask_Bx1xS2_ik1': mask_Bx1xS2_ik1, 'L0_xattn_Wq': _L0_xattn_in['Wq'], 'L0_xattn_bq': _L0_xattn_in['bq'], 'L0_xattn_Wk': _L0_xattn_in['Wk'], 'L0_xattn_bk': _L0_xattn_in['bk'], 'L0_xattn_Wv': _L0_xattn_in['Wv'], 'L0_xattn_bv': _L0_xattn_in['bv'], 'L0_xattn_Wo': _L0_xattn_in['Wo'], 'L0_xattn_bo': _L0_xattn_in['bo'], 'L0_xattn_g0': _L0_xattn_in['g0'], 'L0_xattn_beta0': _L0_xattn_in['beta0'], 'L0_ffn_gate_w': _L0_ffn_in['gate_w'], 'L0_ffn_gate_b': _L0_ffn_in['gate_b'], 'L0_ffn_rw1': _L0_ffn_in['rw1'], 'L0_ffn_rb1': _L0_ffn_in['rb1'], 'L0_ffn_rw2': _L0_ffn_in['rw2'], 'L0_ffn_rb2': _L0_ffn_in['rb2'], 'L0_ffn_rw3': _L0_ffn_in['rw3'], 'L0_ffn_rb3': _L0_ffn_in['rb3'], 'L0_ffn_sw1': _L0_ffn_in['sw1'], 'L0_ffn_sb1': _L0_ffn_in['sb1'], 'L0_ffn_sw2': _L0_ffn_in['sw2'], 'L0_ffn_sb2': _L0_ffn_in['sb2'], 'L0_ffn_sw3': _L0_ffn_in['sw3'], 'L0_ffn_sb3': _L0_ffn_in['sb3'], 'L1_xattn_Wq': _L1_xattn_in['Wq'], 'L1_xattn_Wk': _L1_xattn_in['Wk'], 'L1_xattn_Wv': _L1_xattn_in['Wv'], 'L1_xattn_Wo': _L1_xattn_in['Wo'], 'L1_ffn_W': _L1_ffn_in['W'], 'L1_ffn_b': _L1_ffn_in['b'], 'L1_ffn_V_r': _L1_ffn_in['V_r'], 'L1_ffn_C': _L1_ffn_in['C']}

def reference(x, ctx_1024, mask_Bx1xS2_ik1, L0_xattn_Wq, L0_xattn_bq, L0_xattn_Wk, L0_xattn_bk, L0_xattn_Wv, L0_xattn_bv, L0_xattn_Wo, L0_xattn_bo, L0_xattn_g0, L0_xattn_beta0, L0_ffn_gate_w, L0_ffn_gate_b, L0_ffn_rw1, L0_ffn_rb1, L0_ffn_rw2, L0_ffn_rb2, L0_ffn_rw3, L0_ffn_rb3, L0_ffn_sw1, L0_ffn_sb1, L0_ffn_sw2, L0_ffn_sb2, L0_ffn_sw3, L0_ffn_sb3, L1_xattn_Wq, L1_xattn_Wk, L1_xattn_Wv, L1_xattn_Wo, L1_ffn_W, L1_ffn_b, L1_ffn_V_r, L1_ffn_C):
    import jax
    import jax.numpy as jnp

    def _L0_xattn_ref(Q, K, V, pad_mask, Wq, bq, Wk, bk, Wv, bv, Wo, bo, g0, beta0):
        import jax, jax.numpy as jnp
        import numpy as np
        B, NQ, NK = (8, 512, 512)
        DQ = DK = DV = 256
        EPS = 1e-05

        def _xavier(key, shape):
            fan_in, fan_out = (shape[0], shape[1])
            lim = float(np.sqrt(6.0 / (fan_in + fan_out)))
            return jax.random.uniform(key, shape, jnp.float32, -lim, lim)

        def _layernorm(x, g, b):
            mu = jnp.mean(x, axis=-1, keepdims=True)
            var = jnp.mean(jnp.square(x - mu), axis=-1, keepdims=True)
            return (x - mu) * jax.lax.rsqrt(var + EPS) * g + b
        q = Q @ Wq + bq
        k = K @ Wk + bk
        v = V @ Wv + bv
        scale = 1.0 / jnp.sqrt(jnp.float32(DV))
        scores = jnp.einsum('bqd,bkd->bqk', q, k) * scale
        scores = jnp.where(pad_mask == 0, jnp.float32(-1000000000.0), scores)
        w = jax.nn.softmax(scores, axis=-1)
        out = jnp.einsum('bqk,bkd->bqd', w, v)
        out = out @ Wo + bo
        out = _layernorm(out, g0, beta0)
        return out

    def _L0_ffn_ref(x, gate_w, gate_b, rw1, rb1, rw2, rb2, rw3, rb3, sw1, sb1, sw2, sb2, sw3, sb3):
        import jax, jax.numpy as jnp
        import numpy as np
        B, T, D, H = (4, 512, 256, 512)
        E, S, K = (8, 2, 2)

        def _swiglu_stacked(x, w1, b1, w2, b2, w3, b3):
            p1 = jnp.einsum('btd,ndh->nbth', x, w1) + b1[:, None, None, :]
            p2 = jnp.einsum('btd,ndh->nbth', x, w2) + b2[:, None, None, :]
            glu = jax.nn.silu(p1) * p2
            return jnp.einsum('nbth,nhd->nbtd', glu, w3) + b3[:, None, None, :]
        scores = jax.nn.softmax(x @ gate_w + gate_b, axis=-1)
        weights, indices = jax.lax.top_k(scores, K)
        routed_all = _swiglu_stacked(x, rw1, rb1, rw2, rb2, rw3, rb3)
        out_bted = jnp.transpose(routed_all, (1, 2, 0, 3))
        gathered = jnp.take_along_axis(out_bted, indices[..., None], axis=2)
        routed = jnp.sum(weights[..., None] * gathered, axis=2)
        shared = _swiglu_stacked(x, sw1, sb1, sw2, sb2, sw3, sb3).mean(axis=0)
        return shared + routed

    def _L1_xattn_ref(queries, keys, values, Wq, Wk, Wv, Wo):
        import jax, jax.numpy as jnp
        import numpy as np
        B, S, D, H = (2, 512, 256, 16)
        HD = D // H

        def split_heads(x):
            b, s, _ = x.shape
            return x.reshape(b, s, H, HD).transpose(0, 2, 1, 3)
        q = split_heads(queries @ Wq.T)
        k = split_heads(keys @ Wk.T)
        v = split_heads(values @ Wv.T)
        scale = 1.0 / jnp.sqrt(jnp.asarray(HD, q.dtype))
        scores = jnp.einsum('bhqd,bhkd->bhqk', q, k) * scale
        attn = jax.nn.softmax(scores, axis=-1)
        ctx = jnp.einsum('bhqk,bhkd->bhqd', attn, v)
        out = ctx.transpose(0, 2, 1, 3).reshape(queries.shape[0], -1, D)
        return out @ Wo.T

    def _L1_ffn_ref(x, W, b, V_r, C):
        import jax, jax.numpy as jnp
        import numpy as np
        base = jnp.einsum('bsd,od->bso', x, W) + b
        correction = jnp.einsum('bsr,or->bso', jnp.einsum('bsd,dr->bsr', x, V_r), C)
        return base + correction
    x = x + _L0_xattn_ref(_layernorm(x, axis=-1), ctx_1024, ctx_1024, mask_Bx1xS2_ik1, L0_xattn_Wq, L0_xattn_bq, L0_xattn_Wk, L0_xattn_bk, L0_xattn_Wv, L0_xattn_bv, L0_xattn_Wo, L0_xattn_bo, L0_xattn_g0, L0_xattn_beta0)
    x = x + _L0_ffn_ref(_layernorm(x, axis=-1), L0_ffn_gate_w, L0_ffn_gate_b, L0_ffn_rw1, L0_ffn_rb1, L0_ffn_rw2, L0_ffn_rb2, L0_ffn_rw3, L0_ffn_rb3, L0_ffn_sw1, L0_ffn_sb1, L0_ffn_sw2, L0_ffn_sb2, L0_ffn_sw3, L0_ffn_sb3)
    x = x + _L1_xattn_ref(_layernorm(x, axis=-1), ctx_1024, ctx_1024, L1_xattn_Wq, L1_xattn_Wk, L1_xattn_Wv, L1_xattn_Wo)
    x = x + _L1_ffn_ref(_layernorm(x, axis=-1), L1_ffn_W, L1_ffn_b, L1_ffn_V_r, L1_ffn_C)
    return x

_drawn_inputs = setup_inputs


def setup_inputs(seed=0):
    import zlib

    import numpy as np

    out = dict(_drawn_inputs(seed))
    spreads = {'L0_xattn_bq': (0.0, 0.303),
     'L0_xattn_bk': (0.0, 2.0),
     'L0_xattn_bv': (0.0, 0.1),
     'L0_xattn_bo': (0.0, 0.1),
     'L0_xattn_g0': (1.0, 0.2),
     'L0_xattn_beta0': (0.0, 0.1),
     'L0_ffn_gate_b': (0.0, 0.762),
     'L0_ffn_rb1': (0.0, 0.8),
     'L0_ffn_rb2': (0.0, 0.8),
     'L0_ffn_rb3': (0.0, 1.457),
     'L0_ffn_sb1': (0.0, 0.8),
     'L0_ffn_sb2': (0.0, 0.8),
     'L0_ffn_sb3': (0.0, 0.8)}
    factors = {'L0_ffn_gate_w': 3.688,
     'L0_ffn_rw1': 8.0,
     'L0_ffn_rw2': 8.0,
     'L0_ffn_rw3': 8.0,
     'L0_ffn_sw1': 4.589,
     'L0_ffn_sw2': 4.569,
     'L0_ffn_sw3': 4.323,
     'L1_xattn_Wq': 47.522,
     'L1_xattn_Wk': 46.695,
     'L1_ffn_b': 57.282,
     'L1_xattn_Wv': 5.135,
     'L1_xattn_Wo': 5.125}
    for name, (base, spread) in spreads.items():
        noise = np.random.default_rng([zlib.crc32(name.encode()), seed]).standard_normal(out[name].shape)
        drawn = base * np.exp(spread * noise) if base else spread * noise
        out[name] = jnp.asarray(drawn.astype(out[name].dtype))
    for name, factor in factors.items():
        out[name] = (out[name] * factor).astype(out[name].dtype)
    return out
```

```python
from contextlib import ExitStack

import concourse.bass as bass
from concourse import mybir

F32 = mybir.dt.float32
BF16 = mybir.dt.bfloat16
I32 = mybir.dt.int32
ALU = mybir.AluOpType
AX_X = mybir.AxisListType.X
ACT = mybir.ActivationFunctionType

P = 128
B, S, D = 16, 112, 256
K = 375
KP = K + 1
KC = 125
NKC = K // KC
C = D // P
G = 4
NG = B // G
GS = G * S
E, SE, H = 8, 2, 512
HM = H // P
NH, HD = 16, 16
NT_E = B * S // P
NTILE = 2 * B * S // P + E
EPS = 1e-5
NEG = -1e9


class Count:

    def __init__(self, turn=0, per=0, base=0):
        self.turn, self.per, self.base, self.n = turn, per, base, 0

    def __call__(self, n=1):
        self.n += n
        return self.now()

    def now(self):
        return self.turn * self.per + (self.base + self.n)


def wait_alone(eng, always, semaphore, value):
    value = eng.to_reg(value)
    eng.wait_ge(always, 1)
    eng.wait_ge(semaphore, value)


def layer0(nc, ctx, dram, x_res, xh_moe, logits, bank, ident, ones, always, semaphores):

    def sb(name, shape, dt=F32):
        return ctx.enter_context(nc.sbuf_tensor(name, shape, dt))

    def sem(name):
        return semaphores.enter_context(nc.semaphore(name))

    wq_t = sb("wq_t", [P, C, D])
    wk_t = sb("wk_t", [P, C, D])
    wv_t = sb("wv_t", [P, C, D])
    wo = sb("wo", [P, C, D])
    wqk = sb("wqk", [P, C, D])
    wvo = sb("wvo", [P, C, D])
    cols = sb("cols", [P, 3, C])
    bqk = sb("bqk", [P, C])
    wqbk = sb("wqbk", [P, C])
    rep = sb("rep", [P, 2, C, S])
    cb = sb("cb", [S, 1])
    bo_row = sb("bo_row", [1, D])
    bo_b = sb("bo_b", [S, D])
    g0_b = sb("g0_b", [S, D])
    beta_b = sb("beta_b", [S, D])
    gw = sb("gw", [P, C, E])
    gb_row = sb("gb_row", [1, E])
    sw1 = sb("sw1", [P, SE, C, H])
    sw2 = sb("sw2", [P, SE, C, H])
    sw3 = sb("sw3", [P, SE, HM, D])
    sb12 = sb("sb12", [P, 2, SE * HM])
    sb3_rows = sb("sb3_rows", [1, SE, D])
    stat = sb("stat", [S, G, 6])
    mv = sb("mv", [S, G, 2])
    rstd = sb("rstd", [S, G])
    mhalf = sb("mhalf", [S, G])
    xh = sb("xh", [S, G, D])
    xhT = sb("xhT", [P, C, GS])
    qT = sb("qT", [P, C, GS])
    cq = sb("cq", [S, G])
    ctxT = sb("ctxT", [P, G, C, KP])
    ctxn = sb("ctxn", [KC, G, NKC, D])
    mask_i = sb("mask_i", [S, G, K], I32)
    drop = sb("drop", [S, G, K])
    keep = sb("keep", [S, G, K])
    add = sb("add", [S, G, K])
    sc = sb("sc", [S, 2, K])
    scm = sb("scm", [S, 2, K])
    mx = sb("mx", [S, G])
    nmx = sb("nmx", [S, G])
    probs = sb("probs", [S, 2, K])
    rsum = sb("rsum", [S, G])
    rrec = sb("rrec", [S, G])
    pT = sb("pT", [KC, 2, NKC * S])
    uT = sb("uT", [P, 2, C * S])
    o_sb = sb("o_sb", [S, G, D])
    silu = sb("silu", [P, 2, GS])
    gluT = sb("gluT", [P, SE * HM, GS])
    zeros = sb("zeros", [P, D])

    s = {n: sem(n) for n in (
        "x_in", "weights_in", "fold_ps", "folded", "ctx_in0", "ctx_in1", "ctx_in2", "ctx_in3", "mask_in0", "mask_in1", "mask_in2", "mask_in3",
        "dve0", "pool0", "mv_ready", "rstd_ready", "xh_ready", "xhT_ps", "xhT_ready", "q_ps",
        "q_ready", "c_ps", "s_ps", "s_read", "keep_ready", "max_ready", "p_ready", "pT_ps", "pT_ready",
        "u_ps", "uT_ready", "o_ps", "o_read", "mv1_ready", "rstd1_ready", "mv2_ready", "rstd2_ready",
        "xh1_ready", "xh1T_ps", "xh1T_ready", "gate_ps", "gate_read", "p12_ps", "silu_ready",
        "glu_ready", "sh_ps", "sh_read", "consts_ready", "consts_in", "xh_kept", "shared_in", "zeros_ready", "zeroed")}
    ctx_in = [s[f"ctx_in{j}"] for j in range(G)]
    psum_T = bank[0:2]
    psum_q = bank[2:4]
    psum_s = bank[4:6]
    psum_pT, psum_u = bank[6], bank[7]

    block = ctx.enter_context(nc.Block())

    @block.sync
    def _(sp):
        sp.dma_start(x_res[:], dram["x"].rearrange("b s d -> s b d")).then_inc(s["x_in"], 16)
        for dst, name in ((wq_t, "wq_t"), (wk_t, "wk_t"), (wv_t, "wv_t"), (wo, "wo0")):
            sp.dma_start(dst[:], dram[name].rearrange("(c p) n -> p c n", p=P)).then_inc(s["weights_in"], 16)
        sp.dma_start(cols[:], dram["qkv_bias"]).then_inc(s["weights_in"], 16)
        sp.dma_start(bo_row[:], dram["bo"].rearrange("(o n) -> o n", o=1)).then_inc(s["weights_in"], 16)
        for dst, name in ((g0_b, "g0"), (beta_b, "beta0")):
            sp.dma_start(dst[:], dram[name].rearrange("(o n) -> o n", o=1).to_broadcast([S, D])).then_inc(s["weights_in"], 16)
        sp.dma_start(gw[:], dram["gate_w"].rearrange("(c p) n -> p c n", p=P)).then_inc(s["weights_in"], 16)
        sp.dma_start(gb_row[:], dram["gate_b"].rearrange("(o n) -> o n", o=1)).then_inc(s["weights_in"], 16)
        sp.dma_start(sb12[:], dram["sb12"]).then_inc(s["weights_in"], 16)
        sp.dma_start(sb3_rows[:], dram["sb3"].rearrange("(o e) n -> o e n", o=1)).then_inc(s["weights_in"], 16)
        sp.wait_ge(s["zeros_ready"], 1)
        sp.dma_start(dram["xg"].rearrange("(p r) d -> p r d", p=P), zeros[:].unsqueeze(1).to_broadcast([P, NTILE, D])).then_inc(s["zeroed"], 16)
        with sp.Fori(0, NG) as i:
            for j in range(G):
                b = i * G + j
                sp.wait_ge(s["u_ps"], i * G + (j + 1))
                sp.dma_start(ctxT[:, j, :, :], dram["ctx_t"][b].rearrange("(c p) k -> p c k", p=P)).then_inc(ctx_in[j], 16)
                sp.dma_start(ctxn[:, j, :, :], dram["ctx"][b].rearrange("(c p) d -> p c d", p=KC)).then_inc(ctx_in[j], 16)
                sp.wait_ge(s["keep_ready"], i * G + (j + 1))
                sp.dma_start(mask_i[:, j, :], dram["mask"][b].to_broadcast([S, K])).then_inc(s[f"mask_in{j}"], 16)
        sp.wait_ge(s["zeroed"], 16)

    @block.gpsimd
    def _(pool):
        for dst, name in ((sw1, "sw1"), (sw2, "sw2"), (sw3, "sw3")):
            pool.dma_start(dst[:], dram[name].rearrange("e (c p) n -> p e c n", p=P)).then_inc(s["shared_in"], 16)
        pool.memset(zeros[:], 0.0).then_inc(s["zeros_ready"], 1)
        pool.memset(mhalf[:], -0.5).then_inc(s["pool0"], 1)
        pool.wait_ge(s["pool0"], 1)
        pool.sem_inc(s["keep_ready"], G)
        pool.sem_inc(s["xh_kept"], 1)
        pc = 1

        def power(pool, mean_var, ready, n, done, pbase):
            wait_alone(pool, always, ready, n)
            pool.tensor_scalar(rstd[:], mean_var[:, :, 1], EPS, None, ALU.add).then_inc(s["pool0"], 1)
            wait_alone(pool, always, s["pool0"], pbase)
            pool.tensor_tensor(rstd[:], rstd[:], mhalf[:], ALU.pow).then_inc(done, 1)

        with pool.Fori(0, NG) as i:
            per = 3 + G
            power(pool, mv, s["mv_ready"], i + 1, s["rstd_ready"], i * per + (pc + 1))
            for j in range(G):
                wait_alone(pool, always, s[f"mask_in{j}"], (i + 1) * 16)
                if j == 0:
                    wait_alone(pool, always, s["max_ready"], i * G + G)
                pool.tensor_scalar(drop[:, j, :], mask_i[:, j, :], 0.0, None, ALU.is_equal).then_inc(s["pool0"], 1)
                wait_alone(pool, always, s["pool0"], i * per + (pc + 2 + j))
                pool.tensor_scalar(add[:, j, :], drop[:, j, :], NEG, None, ALU.mult)
                pool.tensor_scalar(keep[:, j, :], drop[:, j, :], -1.0, 1.0, ALU.mult, ALU.add).then_inc(s["keep_ready"], 1)
            power(pool, mv, s["mv1_ready"], i + 1, s["rstd1_ready"], i * per + (pc + 2 + G))
            power(pool, mv, s["mv2_ready"], i + 1, s["rstd2_ready"], i * per + (pc + 3 + G))
            wait_alone(pool, always, s["xh1_ready"], i * G + G)
            pool.tensor_copy(xh_moe[:, bass.ds(i * G, G), :], xh[:]).then_inc(s["xh_kept"], 1)

    @block.vector
    def _(v):
        done = s["dve0"]
        v.sem_inc(s["max_ready"], G)
        v.wait_ge(s["weights_in"], 16 * 12)
        v.wait_ge(s["consts_in"], 32)
        for k in range(2):
            for c in range(C):
                nc.vector.tensor_scalar(rep[:, k, c, :], ones[:, 0:S], cols[:, 2 * k, c:c + 1], None, ALU.mult).then_inc(done, 1)
        v.wait_ge(done, 4)
        v.sem_inc(s["consts_ready"], 1)
        v.wait_ge(s["fold_ps"], 1)
        for c in range(C):
            nc.vector.tensor_scalar(wqk[:, c, :], bank[c][:, 0:D], 1.0 / 16, None, ALU.mult)
            nc.vector.tensor_copy(wvo[:, c, :], bank[2 + c][:, 0:D])
        nc.vector.tensor_scalar(bqk[:], bank[4][:, 0:C], 1.0 / 16, None, ALU.mult)
        nc.vector.tensor_scalar(wqbk[:], bank[4][:, C:2 * C], 1.0 / 16, None, ALU.mult)
        nc.vector.tensor_scalar(cb[:], bank[5][0:S, 0:1], 1.0 / 16, None, ALU.mult)
        nc.vector.tensor_copy(bo_b[:], bank[6][0:S, 0:D]).then_inc(s["folded"], 1)
        v.wait_ge(s["folded"], 1)
        v.wait_ge(s["x_in"], 16)
        PER = 8 * G + 1
        with v.Fori(0, NG) as i:
            n = Count(i, PER, 4)

            def mean_var(src, ready, extra_wait=None):
                for j in range(G):
                    nc.vector.bn_stats(stat[:, j, :], src(j)).then_inc(done, 1)
                    n()
                for j in range(G):
                    wait_alone(v, always, done, n.now() - (G - 1 - j))
                    if j < G - 1:
                        nc.vector.bn_aggr(mv[:, j, :], stat[:, j, :])
                    else:
                        nc.vector.bn_aggr(mv[:, j, :], stat[:, j, :]).then_inc(ready, 1)

            mean_var(lambda j: x_res[:, i * G + j, :], s["mv_ready"])
            v.wait_ge(s["mv_ready"], i + 1)
            v.wait_ge(s["rstd_ready"], i + 1)
            v.wait_ge(s["xh_kept"], i + 1)
            for j in range(G):
                nc.vector.tensor_scalar(xh[:, j, :], x_res[:, i * G + j, :], mv[:, j, 0:1], rstd[:, j:j + 1],
                                        ALU.subtract, ALU.mult).then_inc(s["xh_ready"], 1)
            v.wait_ge(s["c_ps"], i + 1)
            nc.vector.tensor_scalar(cq[:], bank[1][0:S, GS:GS + G], cb[:, 0:1], None, ALU.add).then_inc(done, 1)
            n()
            v.wait_ge(done, n.now())

            def scores(j):
                v.wait_ge(s["s_ps"], i * G + (j + 1))
                v.wait_ge(s["keep_ready"], i * G + (j + 1 + G))
                if j >= 2:
                    v.wait_ge(s["p_ready"], i * G + (j - 1))
                nc.vector.scalar_tensor_tensor(sc[:, j % 2, :], psum_s[j % 2][0:S, 0:K], cq[:, j:j + 1],
                                               keep[:, j, :], ALU.add, ALU.mult).then_inc(s["s_read"], 1)
                wait_alone(v, always, s["s_read"], i * G + (j + 1))
                nc.vector.tensor_tensor_reduce(out=scm[:, j % 2, :], in0=sc[:, j % 2, :], in1=add[:, j, :], scale=1.0,
                                               scalar=-3e38, op0=ALU.add, op1=ALU.max,
                                               accum_out=mx[:, j:j + 1]).then_inc(done, 1)
                n()
                v.wait_ge(done, n.now())
                nc.vector.tensor_scalar(nmx[:, j:j + 1], mx[:, j:j + 1], -1.0, None, ALU.mult).then_inc(s["max_ready"], 1)

            def u_out(j):
                v.wait_ge(s["u_ps"], i * G + (j + 1 + G))
                nc.vector.tensor_copy(uT[:, j % 2, :], psum_u[:, 0:C * S]).then_inc(s["uT_ready"], 1)

            def o_out(j):
                v.wait_ge(s["p_ready"], i * G + (j + 1))
                nc.vector.reciprocal(rrec[:, j:j + 1], rsum[:, j:j + 1]).then_inc(done, 1)
                n()
                v.wait_ge(done, n.now())
                v.wait_ge(s["o_ps"], i * G + (j + 1))
                nc.vector.scalar_tensor_tensor(o_sb[:, j, :], psum_T[j % 2][0:S, 0:D], rrec[:, j:j + 1], bo_b[:],
                                               ALU.mult, ALU.add).then_inc(s["o_read"], 1)

            scores(0)
            scores(1)
            scores(2)
            u_out(0)
            scores(3)
            o_out(0)
            for j in range(1, G):
                u_out(j)
                o_out(j)
            wait_alone(v, always, s["o_read"], i * G + G)
            mean_var(lambda j: o_sb[:, j, :], s["mv1_ready"])
            v.wait_ge(s["mv1_ready"], i + 1)
            v.wait_ge(s["rstd1_ready"], i + 1)
            for step in range(3):
                for j in range(G):
                    if step == 0:
                        nc.vector.scalar_tensor_tensor(o_sb[:, j, :], o_sb[:, j, :], mv[:, j, 0:1], g0_b[:],
                                                       ALU.subtract, ALU.mult).then_inc(done, 1)
                    elif step == 1:
                        v.wait_ge(done, n.now() - (G - 1))
                        nc.vector.scalar_tensor_tensor(o_sb[:, j, :], o_sb[:, j, :], rstd[:, j:j + 1], beta_b[:],
                                                       ALU.mult, ALU.add).then_inc(done, 1)
                    else:
                        v.wait_ge(done, n.now() - (G - 1))
                        nc.vector.tensor_tensor(x_res[:, i * G + j, :], x_res[:, i * G + j, :], o_sb[:, j, :],
                                                ALU.add).then_inc(done, 1)
                    n()
            wait_alone(v, always, done, n.now())
            mean_var(lambda j: x_res[:, i * G + j, :], s["mv2_ready"])
            v.wait_ge(s["mv2_ready"], i + 1)
            v.wait_ge(s["rstd2_ready"], i + 1)
            for j in range(G):
                nc.vector.tensor_scalar(xh[:, j, :], x_res[:, i * G + j, :], mv[:, j, 0:1], rstd[:, j:j + 1],
                                        ALU.subtract, ALU.mult).then_inc(s["xh1_ready"], 1)
            v.wait_ge(s["gate_ps"], i + 1)
            nc.vector.tensor_copy(logits[:, bass.ds(i * G, G), :], bank[6][0:S, 0:G * E].rearrange("p (g e) -> p g e", g=G)).then_inc(s["gate_read"], 1)
            for m in range(SE * HM):
                v.wait_ge(s["silu_ready"], i * (SE * HM) + (m + 1))
                nc.vector.scalar_tensor_tensor(gluT[:, m, :], bank[3 + 2 * (m % 2)][:, 0:GS], sb12[:, 1, m:m + 1],
                                               silu[:, m % 2, :], ALU.add, ALU.mult).then_inc(s["glu_ready"], 1)
            for j in range(G):
                v.wait_ge(s["sh_ps"], i * G + (j + 1))
                nc.vector.scalar_tensor_tensor(x_res[:, i * G + j, :], bank[7 - j % 2][0:S, 0:D], 1.0 / SE,
                                               x_res[:, i * G + j, :], ALU.mult, ALU.add).then_inc(s["sh_read"], 1)
            assert n.n == PER

    @block.scalar
    def _(a):
        a.dma_start(ident[:], dram["identity"]).then_inc(s["consts_in"], 16)
        a.dma_start(ones[:], dram["ones"]).then_inc(s["consts_in"], 16)
        a.wait_ge(s["folded"], 1)
        with a.Fori(0, NG) as i:
            for c in range(C):
                a.wait_ge(s["xhT_ps"], i * C + (c + 1))
                nc.scalar.activation(xhT[:, c, :], psum_T[c][:, 0:GS], ACT.Identity).then_inc(s["xhT_ready"], 1)
            for m in range(C):
                a.wait_ge(s["q_ps"], i * C + (m + 1))
                nc.scalar.activation(qT[:, m, :], psum_q[m][:, 0:GS], ACT.Identity, bias=bqk[:, m:m + 1]).then_inc(s["q_ready"], 1)

            def exps(j):
                a.wait_ge(s["max_ready"], i * G + (j + 1 + G))
                nc.scalar.activation(probs[:, j % 2, :], scm[:, j % 2, :], ACT.Exp, bias=nmx[:, j:j + 1],
                                     accum_out=rsum[:, j:j + 1]).then_inc(s["p_ready"], 1)

            def p_out(j):
                a.wait_ge(s["pT_ps"], i * G + (j + 1))
                if j >= 2:
                    a.wait_ge(s["u_ps"], i * G + (j - 1 + G))
                nc.scalar.activation(pT[:, j % 2, :], psum_pT[0:KC, 0:NKC * S], ACT.Identity).then_inc(s["pT_ready"], 1)

            exps(0)
            exps(1)
            for j in range(G):
                p_out(j)
                if j + 2 < G:
                    exps(j + 2)
            for c in range(C):
                a.wait_ge(s["xh1T_ps"], i * C + (c + 1))
                nc.scalar.activation(xhT[:, c, :], psum_T[c][:, 0:GS], ACT.Identity).then_inc(s["xh1T_ready"], 1)
            for m in range(SE * HM):
                a.wait_ge(s["p12_ps"], i * (SE * HM) + (m + 1))
                if m >= 2:
                    a.wait_ge(s["glu_ready"], i * (SE * HM) + (m - 1))
                nc.scalar.activation(silu[:, m % 2, :], bank[2 + 2 * (m % 2)][:, 0:GS], ACT.Silu,
                                     bias=sb12[:, 0, m:m + 1]).then_inc(s["silu_ready"], 1)

    @block.tensor
    def _(t):
        mm = nc.tensor.matmul
        t.sem_inc(s["u_ps"], G)
        t.wait_ge(s["weights_in"], 16 * 12)
        t.wait_ge(s["shared_in"], 48)
        t.wait_ge(s["consts_in"], 32)
        t.wait_ge(s["consts_ready"], 1)
        for c in range(C):
            for k in range(C):
                mm(bank[c][:, 0:D], wq_t[:, k, c * P:(c + 1) * P], wk_t[:, k, :], start=k == 0, stop=k == C - 1)
            for k in range(C):
                mm(bank[2 + c][:, 0:D], wv_t[:, k, c * P:(c + 1) * P], wo[:, k, :], start=k == 0, stop=k == C - 1)
        for c in range(C):
            for k in range(C):
                mm(bank[4][:, c:c + 1], wk_t[:, k, c * P:(c + 1) * P], cols[:, 0, k:k + 1], start=k == 0, stop=k == C - 1)
        for c in range(C):
            for k in range(C):
                mm(bank[4][:, C + c:C + c + 1], wq_t[:, k, c * P:(c + 1) * P], cols[:, 1, k:k + 1], start=k == 0, stop=k == C - 1)
        for k in range(C):
            mm(bank[5][0:S, 0:1], rep[:, 0, k, :], cols[:, 1, k:k + 1], start=k == 0, stop=k == C - 1)
        for k in range(C):
            mm(bank[6][0:S, 0:D], rep[:, 1, k, :], wo[:, k, :], start=k == 0, stop=False)
        mm(bank[6][0:S, 0:D], ones[0:1, 0:S], bo_row[:], start=False, stop=True).then_inc(s["fold_ps"], 1)
        t.wait_ge(s["folded"], 1)
        with t.Fori(0, NG) as i:
            t.wait_ge(s["xh_ready"], i * G + G)
            for c in range(C):
                for j in range(G):
                    last = nc.tensor.transpose(psum_T[c][:, j * S:(j + 1) * S], xh[:, j, c * P:(c + 1) * P], ident[0:S, 0:S])
                last.then_inc(s["xhT_ps"], 1)
            t.wait_ge(s["xhT_ready"], i * C + C)
            for m in range(C):
                for c in range(C):
                    last = mm(psum_q[m][:, 0:GS], wqk[:, c, m * P:(m + 1) * P], xhT[:, c, :], start=c == 0, stop=c == C - 1)
                last.then_inc(s["q_ps"], 1)
            for j in range(G):
                for c in range(C):
                    last = mm(psum_T[1][0:S, GS + j:GS + j + 1], xhT[:, c, j * S:(j + 1) * S], wqbk[:, c:c + 1], start=c == 0, stop=c == C - 1)
            last.then_inc(s["c_ps"], 1)
            t.wait_ge(s["q_ready"], i * C + C)

            def scores(j):
                t.wait_ge(ctx_in[j], (i + 1) * 32)
                if j >= 2:
                    t.wait_ge(s["s_read"], i * G + (j - 1))
                for c in range(C):
                    last = mm(psum_s[j % 2][0:S, 0:K], qT[:, c, j * S:(j + 1) * S], ctxT[:, j, c, 0:K], start=c == 0, stop=c == C - 1)
                last.then_inc(s["s_ps"], 1)

            def p_T(j):
                t.wait_ge(s["p_ready"], i * G + (j + 1))
                for k in range(NKC):
                    last = nc.tensor.transpose(psum_pT[0:KC, k * S:(k + 1) * S], probs[:, j % 2, k * KC:(k + 1) * KC], ident[0:S, 0:S])
                last.then_inc(s["pT_ps"], 1)

            def u(j):
                t.wait_ge(s["pT_ready"], i * G + (j + 1))
                for m in range(C):
                    for k in range(NKC):
                        last = mm(psum_u[:, m * S:(m + 1) * S], ctxn[:, j, k, m * P:(m + 1) * P], pT[:, j % 2, k * S:(k + 1) * S],
                                  start=k == 0, stop=k == NKC - 1)
                last.then_inc(s["u_ps"], 1)

            def o(j):
                t.wait_ge(s["uT_ready"], i * G + (j + 1))
                if j >= 2:
                    t.wait_ge(s["o_read"], i * G + (j - 1))
                for c in range(C):
                    last = mm(psum_T[j % 2][0:S, 0:D], uT[:, j % 2, c * S:(c + 1) * S], wvo[:, c, :], start=c == 0, stop=c == C - 1)
                last.then_inc(s["o_ps"], 1)

            scores(0)
            scores(1)
            p_T(0)
            scores(2)
            u(0)
            p_T(1)
            o(0)
            scores(3)
            for j in range(1, G):
                u(j)
                if j + 1 < G:
                    p_T(j + 1)
                o(j)
            t.wait_ge(s["xh1_ready"], i * G + G)
            for c in range(C):
                for j in range(G):
                    last = nc.tensor.transpose(psum_T[c][:, j * S:(j + 1) * S], xh[:, j, c * P:(c + 1) * P], ident[0:S, 0:S])
                last.then_inc(s["xh1T_ps"], 1)
            t.wait_ge(s["xh1T_ready"], i * C + C)
            for j in range(G):
                for c in range(C):
                    mm(bank[6][0:S, j * E:(j + 1) * E], xhT[:, c, j * S:(j + 1) * S], gw[:, c, :], start=c == 0, stop=False)
                last = mm(bank[6][0:S, j * E:(j + 1) * E], ones[0:1, 0:S], gb_row[:], start=False, stop=True)
            last.then_inc(s["gate_ps"], 1)
            for m in range(SE * HM):
                e, h = divmod(m, HM)
                if m >= 2:
                    t.wait_ge(s["glu_ready"], i * (SE * HM) + (m - 1))
                for k, w in enumerate((sw1, sw2)):
                    for c in range(C):
                        last = mm(bank[2 + 2 * (m % 2) + k][:, 0:GS], w[:, e, c, h * P:(h + 1) * P], xhT[:, c, :], start=c == 0, stop=c == C - 1)
                last.then_inc(s["p12_ps"], 1)
            t.wait_ge(s["glu_ready"], i * (SE * HM) + SE * HM)
            t.wait_ge(s["gate_read"], i + 1)
            for j in range(G):
                if j >= 2:
                    t.wait_ge(s["sh_read"], i * G + (j - 1))
                for m in range(SE * HM):
                    e, h = divmod(m, HM)
                    mm(bank[7 - j % 2][0:S, 0:D], gluT[:, m, j * S:(j + 1) * S], sw3[:, e, h, :], start=m == 0, stop=False)
                for e in range(SE):
                    last = mm(bank[7 - j % 2][0:S, 0:D], ones[0:1, 0:S], sb3_rows[:, e, :], start=False, stop=e == SE - 1)
                last.then_inc(s["sh_ps"], 1)
    return list(s.values())


def routing_and_projections(nc, ctx, dram, xh_moe, logits, weight1, weight2, slots, expert_row,
                            weights, biases, ps, bank, ones, always, semaphores):

    def sb(name, shape, dt=F32):
        return ctx.enter_context(nc.sbuf_tensor(name, shape, dt))

    def sem(name):
        return semaphores.enter_context(nc.semaphore(name))

    TE = B * E
    before = sb("before", [S, S])
    iota = sb("iota", [S, E])
    lower = sb("lower", [S, E, E])
    steps = sb("steps", [S, NT_E])
    tiles = sb("tiles", [S, NTILE])
    top = sb("top", [S, B])
    gates = sb("gates", [S, B, E])
    hit = sb("hit", [S, B, E])
    cand = sb("cand", [S, B, E])
    index = sb("index", [S, B])
    one1 = sb("one1", [S, B, E])
    one2 = sb("one2", [S, B, E])
    both = sb("both", [S, 2 * B, E])
    count = sb("count", [S, E])
    over = sb("over", [S, E, NT_E])
    ntile = sb("ntile", [S, E])
    prod = sb("prod", [S, E, E])
    first = sb("first", [S, E])
    first128 = sb("first128", [S, E])
    slot = gates
    slot_f = sb("slot_f", [S, 2, B])
    started = sb("started", [S, E - 1, NTILE])
    expert_f = sb("expert_f", [S, NTILE])
    wk1 = sb("wk1", [P, C, D])
    wv1 = sb("wv1", [P, C, D])
    cT = sb("cT", [P, 2, C, KP])
    ka = sb("ka", [P, 2, 3, C, KP], BF16)
    kr = sb("kr", [P, 2, C, KP])
    va = sb("va", [KC, 2, NKC, NH, HD + 1])

    s = {n: sem("b_" + n) for n in (
        "consts_in", "weights_in", "ctx_in0", "ctx_in1", "dve", "sub_ready", "exp_ready", "both_ready",
        "pos_ps", "slots_ready", "scattered", "k_ps", "k_read", "k1_ready", "r_ready", "k2_ready", "k3_ready",
        "v_ps", "v_ready", "k_out0", "k_out1", "v_out0", "v_out1", "ones_ready", "experts_in")}
    block = ctx.enter_context(nc.Block())
    kscr, vscr, xg = dram["kscr"], dram["vscr"], dram["xg"]

    @block.sync
    def _(sp):
        for dst, name in ((before, "before"), (iota, "iota"), (lower, "lower"), (steps, "steps"), (tiles, "tiles")):
            sp.dma_start(dst[:], dram[name]).then_inc(s["consts_in"], 16)
        for dst, name in ((wk1, "wk1_t"), (wv1, "wv1_t")):
            sp.dma_start(dst[:], dram[name].rearrange("(c p) n -> p c n", p=P)).then_inc(s["weights_in"], 16)
        def turn(i, first):
            for q in range(2):
                if not first:
                    sp.wait_ge(s["v_ps"], (i - 1) * 2 + (q + 1))
                sp.dma_start(cT[:, q, :, :], dram["ctx_t"][i * 2 + q].rearrange("(c p) k -> p c k", p=P)).then_inc(s[f"ctx_in{q}"], 16)
            for q in range(2):
                sp.wait_ge(s["v_ready"], i * 2 + (q + 1))
                sp.dma_start(vscr[i * 2 + q], va[:, q, :, :, :].rearrange("p c h d -> p (c h d)")).then_inc(s[f"v_out{q}"], 16)

        turn(0, True)
        with sp.Fori(1, B // 2) as i:
            turn(i, False)
        for q in range(2):
            sp.wait_ge(s[f"v_out{q}"], 16 * (B // 2))

    @block.gpsimd
    def _(pool):
        pool.memset(va[:], 1.0).then_inc(s["ones_ready"], 1)
        pool.wait_ge(s["slots_ready"], 1)
        for k in range(2):
            for t in range(B):
                pool.indirect_dma_start(out=xg, out_offset=bass.IndirectOffsetOnAxis(ap=slots[0:S, k, t:t + 1], axis=0),
                                        in_=xh_moe[:, t, :], in_offset=None).then_inc(s["scattered"], 16)
        pool.wait_ge(s["scattered"], 16 * 2 * B)

    @block.vector
    def _(v):
        done, n = s["dve"], Count()
        V = nc.vector

        def wide(ap):
            return ap.unsqueeze(2).to_broadcast([S, B, E])

        def over_tokens(ap):
            return ap.unsqueeze(1).to_broadcast([S, B, E])

        V.memset(both[:, 0:B, :], 0.0)
        v.wait_ge(s["consts_in"], 16 * 5)
        V.tensor_reduce(top[:], logits[:], axis=AX_X, op=ALU.max).then_inc(done, 1)
        v.wait_ge(done, n())
        V.tensor_tensor(gates[:], logits[:], wide(top[:]), ALU.subtract).then_inc(s["sub_ready"], 1)
        v.wait_ge(s["exp_ready"], 1)
        V.tensor_reduce(top[:], gates[:], axis=AX_X, op=ALU.add).then_inc(done, 1)
        v.wait_ge(done, n())
        V.reciprocal(top[:], top[:]).then_inc(done, 1)
        v.wait_ge(done, n())
        V.tensor_tensor(gates[:], gates[:], wide(top[:]), ALU.mult).then_inc(done, 1)
        v.wait_ge(done, n())
        for weight, one in ((weight1, one1), (weight2, one2)):
            V.tensor_reduce(weight[:], gates[:], axis=AX_X, op=ALU.max).then_inc(done, 1)
            v.wait_ge(done, n())
            V.tensor_tensor(hit[:], gates[:], wide(weight[:]), ALU.is_ge).then_inc(done, 1)
            v.wait_ge(done, n())
            V.tensor_scalar(hit[:], hit[:], -float(E), float(E), ALU.mult, ALU.add).then_inc(done, 1)
            v.wait_ge(done, n())
            V.tensor_tensor(cand[:], hit[:], over_tokens(iota[:]), ALU.add).then_inc(done, 1)
            v.wait_ge(done, n())
            V.tensor_reduce(index[:], cand[:], axis=AX_X, op=ALU.min).then_inc(done, 1)
            v.wait_ge(done, n())
            V.tensor_tensor(one[:], over_tokens(iota[:]), wide(index[:]), ALU.is_equal).then_inc(done, 1)
            v.wait_ge(done, n())
            if one is one1:
                V.scalar_tensor_tensor(gates[:].rearrange("p b e -> p (b e)"), one1[:].rearrange("p b e -> p (b e)"), -2.0,
                                       gates[:].rearrange("p b e -> p (b e)"), ALU.mult, ALU.add).then_inc(done, 1)
                v.wait_ge(done, n())
        V.tensor_tensor(both[:, B:2 * B, :], one1[:], one2[:], ALU.add).then_inc(s["both_ready"], 1)
        v.wait_ge(s["pos_ps"], 1)
        V.tensor_copy(count[:], bank[7][0:S, TE:TE + E]).then_inc(done, 1)
        v.wait_ge(done, n())
        V.tensor_tensor(over[:], count[:].unsqueeze(2).to_broadcast([S, E, NT_E]),
                        steps[:].unsqueeze(1).to_broadcast([S, E, NT_E]), ALU.is_gt).then_inc(done, 1)
        v.wait_ge(done, n())
        V.tensor_reduce(ntile[:], over[:], axis=AX_X, op=ALU.add).then_inc(done, 1)
        v.wait_ge(done, n())
        V.tensor_tensor(prod[:], lower[:], ntile[:].unsqueeze(1).to_broadcast([S, E, E]), ALU.mult).then_inc(done, 1)
        v.wait_ge(done, n())
        V.tensor_reduce(first[:], prod[:], axis=AX_X, op=ALU.add).then_inc(done, 1)
        v.wait_ge(done, n())
        V.tensor_scalar(first128[:], first[:], float(P), None, ALU.mult).then_inc(done, 1)
        v.wait_ge(done, n())
        V.tensor_tensor(slot[:], bank[7][0:S, 0:TE].rearrange("p (b e) -> p b e", e=E), over_tokens(first128[:]), ALU.add).then_inc(done, 1)
        v.wait_ge(done, n())
        for k, one in enumerate((one1, one2)):
            V.tensor_tensor(cand[:], one[:], slot[:], ALU.mult).then_inc(done, 1)
            v.wait_ge(done, n())
            V.tensor_reduce(slot_f[:, k, :], cand[:], axis=AX_X, op=ALU.add).then_inc(done, 1)
            v.wait_ge(done, n())
        V.tensor_copy(slots[:], slot_f[:]).then_inc(s["slots_ready"], 1)
        V.tensor_tensor(started[:], tiles[:].unsqueeze(1).to_broadcast([S, E - 1, NTILE]),
                        first[:, 1:E].unsqueeze(2).to_broadcast([S, E - 1, NTILE]), ALU.is_ge).then_inc(done, 1)
        v.wait_ge(done, n())
        V.tensor_reduce(expert_f[:], started[:].rearrange("p e t -> p t e"), axis=AX_X, op=ALU.add).then_inc(done, 1)
        v.wait_ge(done, n())
        V.tensor_copy(expert_row[:], expert_f[0:1, :]).then_inc(done, 1)
        n()
        def turn(i):
            for q in range(2):
                at = i * 2 + (q + 1)
                v.wait_ge(s["k1_ready"], at)
                V.tensor_tensor(kr[:, q, :, :], ps[:, 2 * q:2 * q + 2, 0:KP], ka[:, q, 0, :, :], ALU.subtract).then_inc(s["k_read"], 1)
                v.wait_ge(s["k_read"], at)
                V.tensor_copy(ka[:, q, 1, :, :], kr[:, q, :, :]).then_inc(s["k2_ready"], 1)
                v.wait_ge(s["k2_ready"], at)
                V.tensor_tensor(ka[:, q, 2, :, :], kr[:, q, :, :], ka[:, q, 1, :, :], ALU.subtract).then_inc(s["k3_ready"], 1)

        with v.Fori(0, B // 2) as i:
            turn(i)

    @block.scalar
    def _(a):
        a.wait_ge(s["sub_ready"], 1)
        nc.scalar.activation(gates[:], gates[:], ACT.Exp).then_inc(s["exp_ready"], 1)
        a.wait_ge(s["ones_ready"], 1)
        def turn(i, first):
            for dst, name in zip(weights, ("rw1", "rw2", "rw3")):
                a.dma_start(dst[:, i, :, :], dram[name][i].rearrange("(c p) n -> p c n", p=P)).then_inc(s["experts_in"], 16)
            for q in range(2):
                at = i * 2 + (q + 1)
                a.wait_ge(s["k_ps"], at)
                if not first:
                    a.wait_ge(s[f"k_out{q}"], i * 32)
                nc.scalar.activation(ka[:, q, 0, :, :], ps[:, 2 * q:2 * q + 2, 0:KP], ACT.Copy).then_inc(s["k1_ready"], 1)
                a.wait_ge(s["v_ps"], at)
                if not first:
                    a.wait_ge(s[f"v_out{q}"], i * 16)
                nc.scalar.activation(va[:, q, 0:2, :, 0:HD],
                                     ps[0:KC, 4 + 2 * q, :].rearrange("p (c h d) -> p c h d", c=2, d=HD), ACT.Copy)
                nc.scalar.activation(va[:, q, 2, :, 0:HD],
                                     ps[0:KC, 5 + 2 * q, 0:D].rearrange("p (h d) -> p h d", d=HD), ACT.Copy).then_inc(s["v_ready"], 1)
            for q in range(2):
                a.wait_ge(s["k3_ready"], i * 2 + (q + 1))
                for m in range(C):
                    a.dma_start(kscr[i * 2 + q][:, m * P:(m + 1) * P, :].rearrange("s f k -> f s k"), ka[:, q, :, m, :]).then_inc(s[f"k_out{q}"], 16)

        for dst, name in zip(biases, ("rb1", "rb2", "rb3")):
            a.dma_start(dst[:], dram[name].rearrange("(o e) n -> o e n", o=1).to_broadcast([P, E, dst.shape[2]])).then_inc(s["experts_in"], 16)
        turn(0, True)
        with a.Fori(1, B // 2) as i:
            turn(i, False)
        a.wait_ge(s["experts_in"], 16 * 3 * (E + 1))
        for q in range(2):
            a.wait_ge(s[f"k_out{q}"], 32 * (B // 2))

    @block.tensor
    def _(t):
        mm = nc.tensor.matmul
        t.wait_ge(s["weights_in"], 32)
        t.wait_ge(s["consts_in"], 16 * 5)
        t.wait_ge(s["both_ready"], 1)
        row = both[:].rearrange("p b e -> p (b e)")
        mm(bank[7][0:S, 0:TE], before[:], row[:, TE:2 * TE], start=True, stop=False)
        for k in range(1, B):
            last = mm(bank[7][0:S, 0:TE], ones[0:S, 0:S], row[:, TE - k * E:2 * TE - k * E], start=False, stop=k == B - 1)
        for k in range(B):
            last = mm(bank[7][0:S, TE:TE + E], ones[0:S, 0:S], row[:, TE + k * E:TE + (k + 1) * E], start=k == 0, stop=k == B - 1)
        last.then_inc(s["pos_ps"], 1)

        def turn(i, first):
            for q in range(2):
                t.wait_ge(s[f"ctx_in{q}"], (i + 1) * 16)
                if not first:
                    t.wait_ge(s["k_read"], (i - 1) * 2 + (q + 1))
                for m in range(C):
                    for c in range(C):
                        last = mm(ps[:, 2 * q + m, 0:KP], wk1[:, c, m * P:(m + 1) * P], cT[:, q, c, :], start=c == 0, stop=c == C - 1)
                last.then_inc(s["k_ps"], 1)
                if not first:
                    t.wait_ge(s["v_ready"], (i - 1) * 2 + (q + 1))
                elif q == 1:
                    t.wait_ge(s["slots_ready"], 1)
                for k in range(NKC):
                    for c in range(C):
                        last = mm(ps[0:KC, 4 + 2 * q + k // 2, (k % 2) * D:(k % 2 + 1) * D], cT[:, q, c, k * KC:(k + 1) * KC], wv1[:, c, :],
                                  start=c == 0, stop=c == C - 1)
                last.then_inc(s["v_ps"], 1)

        turn(0, True)
        with t.Fori(1, B // 2) as i:
            turn(i, False)


def routed_experts(nc, ctx, dram, expert_row, weights, biases, ps, bank, ident, always, semaphores):

    def sb(name, shape, dt=F32):
        return ctx.enter_context(nc.sbuf_tensor(name, shape, dt))

    def sem(name):
        return semaphores.enter_context(nc.semaphore(name))

    rw1, rw2, rw3 = weights
    rb1, rb2, rb3 = biases
    rows = sb("rows", [P, 2, D])
    rowsT = sb("rowsT", [P, 2, C * P])
    h1 = sb("h1", [P, 2, H])
    h2 = sb("h2", [P, 2, H])
    act1 = sb("act1", [P, 2, H])
    glu = sb("glu", [P, 2, H])
    gT = sb("gT", [P, 2, H])
    y = sb("y", [P, 2, D])
    s = {n: sem("c_" + n) for n in (
        "rows_in0", "rows_in1", "rT_ps", "rT_ready", "p1_ps", "p2_ps", "h1_ready", "silu_ready", "h2_ready",
        "glu_ready", "gT_ps", "gT_ready", "y_ps", "y_ready", "y_out0", "y_out1")}
    xg, yscr = dram["xg"], dram["yscr"]
    LAST = NTILE - 1
    block = ctx.enter_context(nc.Block())

    @block.sync
    def _(sp):
        def load(n, q, first=False):
            if not first:
                sp.wait_ge(s["rT_ps"], n - 1)
            sp.dma_start(rows[:, q, :], xg[bass.ds(n * P, P), :]).then_inc(s[f"rows_in{q}"], 16)

        load(0, 0, True)
        load(1, 1, True)
        with sp.Fori(1, NTILE // 2) as i:
            for q in range(2):
                load(i * 2 + q, q)

    @block.gpsimd
    def _(pool):
        with pool.Fori(0, NTILE // 2) as i:
            for q in range(2):
                n = i * 2 + q
                wait_alone(pool, always, s["y_ready"], n + 1)
                pool.dma_start(yscr[bass.ds(n * P, P), :], y[:, q, :]).then_inc(s[f"y_out{q}"], 16)
        for q in range(2):
            pool.wait_ge(s[f"y_out{q}"], 16 * (NTILE // 2))

    @block.vector
    def _(v):
        V = nc.vector

        def expert(n):
            return v.value_load(expert_row[0:1, bass.ds(n, 1)], min_val=0, max_val=E - 1)

        def front(n, q):
            e = expert(n)
            v.wait_ge(s["p1_ps"], n + 1)
            V.tensor_tensor(h1[:, q, :], bank[1 + 2 * q], rb1[:, e, :], ALU.add).then_inc(s["h1_ready"], 1)
            v.wait_ge(s["p2_ps"], n + 1)
            V.tensor_tensor(h2[:, q, :], bank[2 + 2 * q], rb2[:, e, :], ALU.add).then_inc(s["h2_ready"], 1)
            v.wait_ge(s["silu_ready"], n + 1)
            v.wait_ge(s["h2_ready"], n + 1)
            V.tensor_tensor(glu[:, q, :], act1[:, q, :], h2[:, q, :], ALU.mult).then_inc(s["glu_ready"], 1)

        def back(n, q, turn):
            e = expert(n)
            if turn is not None:
                v.wait_ge(s[f"y_out{q}"], turn * 16)
            v.wait_ge(s["y_ps"], n + 1)
            V.tensor_tensor(y[:, q, :], bank[6][:, 0:D], rb3[:, e, :], ALU.add).then_inc(s["y_ready"], 1)

        front(0, 0)
        front(1, 1)
        back(0, 0, None)
        front(2, 0)
        back(1, 1, None)
        with v.Fori(1, NTILE // 2 - 1) as i:
            front(i * 2 + 1, 1)
            back(i * 2, 0, i)
            front(i * 2 + 2, 0)
            back(i * 2 + 1, 1, i)
        front(LAST, 1)
        back(LAST - 1, 0, NTILE // 2 - 1)
        back(LAST, 1, NTILE // 2 - 1)

    @block.scalar
    def _(a):
        A = nc.scalar.activation

        def rowsT_out(n, q):
            a.wait_ge(s["rT_ps"], n + 1)
            A(rowsT[:, q, :], bank[0][:, 0:C * P], ACT.Copy).then_inc(s["rT_ready"], 1)

        def gT_out(n, q):
            a.wait_ge(s["gT_ps"], n + 1)
            A(gT[:, q, :], bank[5], ACT.Copy).then_inc(s["gT_ready"], 1)

        def silu(n, q):
            a.wait_ge(s["h1_ready"], n + 1)
            A(act1[:, q, :], h1[:, q, :], ACT.Silu).then_inc(s["silu_ready"], 1)

        rowsT_out(0, 0)
        rowsT_out(1, 1)
        silu(0, 0)
        with a.Fori(0, NTILE // 2 - 1) as i:
            for k in range(2):
                rowsT_out(i * 2 + 2 + k, k)
                gT_out(i * 2 + k, k)
                silu(i * 2 + 1 + k, 1 - k)
        gT_out(LAST - 1, 0)
        silu(LAST, 1)
        gT_out(LAST, 1)

    @block.tensor
    def _(t):
        mm = nc.tensor.matmul

        def rows_T(n, q, turn):
            t.wait_ge(s[f"rows_in{q}"], (turn + 1) * 16)
            if not (isinstance(n, int) and n == 0):
                t.wait_ge(s["rT_ready"], n)
            for c in range(C):
                last = nc.tensor.transpose(bank[0][:, c * P:(c + 1) * P], rows[:, q, c * P:(c + 1) * P], ident[:])
            last.then_inc(s["rT_ps"], 1)

        def up(n, q):
            e = t.value_load(expert_row[0:1, bass.ds(n, 1)], min_val=0, max_val=E - 1)
            t.wait_ge(s["rT_ready"], n + 1)
            for k, (w, sign) in enumerate(((rw1, "p1_ps"), (rw2, "p2_ps"))):
                for c in range(C):
                    last = mm(bank[1 + 2 * q + k], rowsT[:, q, c * P:(c + 1) * P], w[:, e, c, :], start=c == 0, stop=c == C - 1)
                last.then_inc(s[sign], 1)

        def hidden_T(n, q):
            t.wait_ge(s["glu_ready"], n + 1)
            for m in range(HM):
                last = nc.tensor.transpose(bank[5][:, m * P:(m + 1) * P], glu[:, q, m * P:(m + 1) * P], ident[:])
            last.then_inc(s["gT_ps"], 1)

        def down(n, q):
            e = t.value_load(expert_row[0:1, bass.ds(n, 1)], min_val=0, max_val=E - 1)
            t.wait_ge(s["gT_ready"], n + 1)
            if not (isinstance(n, int) and n == 0):
                t.wait_ge(s["y_ready"], n)
            for m in range(HM):
                last = mm(bank[6][:, 0:D], gT[:, q, m * P:(m + 1) * P], rw3[:, e, m, :], start=m == 0, stop=m == HM - 1)
            last.then_inc(s["y_ps"], 1)

        def step(n, q, turn):
            rows_T(n + 1, 1 - q, turn)
            hidden_T(n - 1, 1 - q)
            up(n, q)
            down(n - 1, 1 - q)

        rows_T(0, 0, 0)
        rows_T(1, 1, 0)
        up(0, 0)
        step(1, 1, 1)
        step(2, 0, 1)
        with t.Fori(1, NTILE // 2 - 1) as i:
            step(i * 2 + 1, 1, i + 1)
            step(i * 2 + 2, 0, i + 1)
        hidden_T(LAST - 1, 0)
        up(LAST, 1)
        down(LAST - 1, 0)
        hidden_T(LAST, 1)
        down(LAST, 1)


def layer1(nc, ctx, dram, out, x_res, weight1, weight2, slots, ps, bank, ident, ones, always, semaphores):

    def sb(name, shape, dt=F32):
        return ctx.enter_context(nc.sbuf_tensor(name, shape, dt))

    def sem(name):
        return semaphores.enter_context(nc.semaphore(name))

    DEPTH = 3 * 2 * HD
    QUAD = 4
    yscr, kscr, vscr, qscr, mscr = (dram[n] for n in ("yscr", "kscr", "vscr", "qscr", "mscr"))
    wq1 = sb("wq1", [P, C, D])
    wo1 = sb("wo1", [P, C, D])
    wf = sb("wf", [P, C, D])
    vrT = sb("vrT", [32, D])
    cfT = sb("cfT", [32, D])
    bf_row = sb("bf_row", [1, D])
    half = sb("half", [S, G])
    yg = sb("yg", [S, G, 2, D])
    stat = sb("d_stat", [S, G, 6])
    mv = sb("d_mv", [S, G, 2])
    rstd = sb("d_rstd", [S, G])
    xh = sb("d_xh", [S, G, D])
    xhT = sb("d_xhT", [P, C, GS])
    qa = sb("qa", [P, 3, C, GS], BF16)
    qr = sb("qr", [P, C, GS])
    kst = sb("kst", [P, 4, NH, KP], BF16)
    qst = sb("qst", [P, 4, NH, S], BF16)
    vt = sb("vt", [KC, 2, NKC, NH, HD + 1])
    mxh = sb("mxh", [S, NH])
    mr = sb("mr", [S, 2, NH])
    mparts = sb("mparts", [S, 2, 3, NH], BF16)
    identb = sb("identb", [P, P], BF16)
    mT = sb("mT", [3 * NH, 2, S], BF16)
    pT = sb("d_pT", [KC, 2, NKC, QUAD * S])
    rec = sb("rec", [S, NH])
    heads = sb("heads", [S, B, D])
    res = sb("res", [S, G, D])

    s = {n: sem("d_" + n) for n in (
        "weights_in", "consts_ready", "half_ready", "wf_ps", "wf_ready", "y_in0", "y_in1", "y_in2", "y_in3", "dve", "pool", "mixed", "mv_ready",
        "rstd_ready", "xh_ready", "xhT_ps", "xhT_ready", "q_ps", "q1_ready", "q_read", "q2_ready", "q3_ready", "q_out",
        "k_in0", "k_in1", "k_in2", "k_in3", "qs_in0", "qs_in1", "qs_in2", "qs_in3", "v_in0", "v_in1",
        "s_ps", "s_max", "m_ready", "mT_ps", "mT_ready", "m_out0", "m_out1", "mrow_in0", "mrow_in1", "mrow_in2", "mrow_in3",
        "st_ps", "p_ready", "pv_ps", "heads_ready", "h_kept", "hT_ps", "hT_ready", "o_ps", "x3_ready",
        "mv3_ready", "rstd3_ready", "xh3_ready", "x3T_ps", "x3T_ready", "f_ps", "res_ready", "res_out0", "res_out1", "res_out2", "res_out3")}
    block = ctx.enter_context(nc.Block())

    def rstd_of(pool, ready, n, done, steps):
        wait_alone(pool, always, ready, n)
        pool.tensor_scalar(rstd[:], mv[:, :, 1], EPS, None, ALU.add).then_inc(s["pool"], 1)
        pool.wait_ge(s["pool"], steps)
        pool.tensor_tensor(rstd[:], rstd[:], half[:], ALU.pow).then_inc(done, 1)

    PAIRS = ((0, 0), (1, 0), (2, 0), (0, 1), (1, 1), (0, 2))

    @block.sync
    def _(sp):
        for dst, name in ((wq1, "wq1_t"), (wo1, "wo1_t"), (wf, "wf_t")):
            sp.dma_start(dst[:], dram[name].rearrange("(c p) n -> p c n", p=P)).then_inc(s["weights_in"], 16)
        for dst, name in ((vrT, "vr_t"), (cfT, "cf_t")):
            sp.dma_start(dst[:], dram[name]).then_inc(s["weights_in"], 16)
        sp.dma_start(bf_row[:], dram["bf"].rearrange("(o n) -> o n", o=1)).then_inc(s["weights_in"], 16)

        def load_keys(b, slot):
            for r, (k, _) in enumerate(PAIRS):
                sp.dma_start(kst[r * HD:(r + 1) * HD, slot, :, :], kscr[b, k].rearrange("(h p) t -> p h t", p=HD)).then_inc(s[f"k_in{slot}"], 16)

        def load_values(b, slot):
            sp.dma_start(vt[:, slot, :, :, :].rearrange("p c h d -> p (c h d)"), vscr[b]).then_inc(s[f"v_in{slot}"], 16)

        for b in range(4):
            load_keys(b, b)
        for b in range(2):
            load_values(b, b)
        with sp.Fori(0, NG) as i:
            sp.wait_ge(s["q3_ready"], i + 1)
            for m in range(C):
                sp.dma_start(qscr[i][:, m * P:(m + 1) * P, :].rearrange("s f t -> f s t"), qa[:, :, m, :]).then_inc(s["q_out"], 16)
            wait_alone(sp, always, s["q_out"], (i + 1) * 32)

        def ahead_in_turn(i, j):
            sp.wait_ge(s["mT_ready"], i * 4 + (j + 1))
            sp.dma_start(mscr[i * 4 + j], mT[:, j % 2, :]).then_inc(s[f"m_out{j % 2}"], 16)
            sp.wait_ge(s[f"m_out{j % 2}"], (i * 2 + (j // 2 + 1)) * 16)
            sp.dma_start(qst[DEPTH:DEPTH + 3, j, :, :], mscr[i * 4 + j].rearrange("(s h) q -> s h q", h=NH)).then_inc(s[f"mrow_in{j}"], 16)

        ahead_in_turn(0, 0)
        ahead_in_turn(0, 1)

        def turn(i, last):
            for j in range(4):
                if j < 2:
                    ahead_in_turn(i, j + 2)
                elif not last:
                    ahead_in_turn(i + 1, j - 2)
                if not last or j < 2:
                    sp.wait_ge(s["pv_ps"], i * 4 + (j + 1))
                    load_values(i * 4 + (j + 2), j % 2)
                if not last:
                    load_keys(i * 4 + (j + 4), j)

        with sp.Fori(0, NG - 1) as i:
            turn(i, False)
        turn(NG - 1, True)
        with sp.Fori(0, NG) as i:
            for j in range(G):
                sp.wait_ge(s["res_ready"], i * G + (j + 1))
                sp.dma_start(out[i * G + j], res[:, j, :]).then_inc(s[f"res_out{j}"], 16)
        for j in range(G):
            sp.wait_ge(s[f"res_out{j}"], 16 * NG)

    @block.gpsimd
    def _(pool):
        pool.memset(half[:], -0.5).then_inc(s["half_ready"], 1)
        pool.wait_ge(s["half_ready"], 1)
        pool.memset(kst[DEPTH:DEPTH + 3, :, :, :], 1.0).then_inc(s["consts_ready"], 1)
        pool.wait_ge(s["consts_ready"], 1)
        for i in range(NG):
            for j in range(G):
                b = i * G + j
                if i:
                    pool.wait_ge(s["mixed"], (i - 1) * G + j + 1)
                for k in range(2):
                    pool.indirect_dma_start(out=yg[:, j, k, :], out_offset=None, in_=yscr,
                                            in_offset=bass.IndirectOffsetOnAxis(ap=slots[0:S, k, b:b + 1], axis=0)).then_inc(s[f"y_in{j}"], 16)
            rstd_of(pool, s["mv_ready"], i + 1, s["rstd_ready"], i + 1)

        def load_queries(i, j):
            for r, (_, k) in enumerate(PAIRS):
                pool.dma_start(qst[r * HD:(r + 1) * HD, j, :, :],
                               qscr[i, k][:, j * S:(j + 1) * S].rearrange("(h p) t -> p h t", p=HD)).then_inc(s[f"qs_in{j}"], 16)

        pool.wait_ge(s["q_out"], NG * 32)
        for j in range(4):
            load_queries(0, j)
        with pool.Fori(0, NG - 1) as i:
            for j in range(4):
                wait_alone(pool, always, s["pv_ps"], i * 4 + (j + 1))
                load_queries(i + 1, j)
        with pool.Fori(0, NG) as i:
            rstd_of(pool, s["mv3_ready"], i + 1, s["rstd3_ready"], i + (NG + 1))

    @block.vector
    def _(v):
        V, done = nc.vector, s["dve"]
        v.wait_ge(s["weights_in"], 16 * 6)
        v.wait_ge(s["wf_ps"], 1)
        V.tensor_tensor(wf[:], wf[:], ps[:, 0:C, 0:D], ALU.add).then_inc(s["wf_ready"], 1)
        V.tensor_copy(identb[:], ident[:]).then_inc(s["wf_ready"], 1)

        def mean_var(src, ready, n):
            for j in range(G):
                V.bn_stats(stat[:, j, :], src(j)).then_inc(done, 1)
                n()
            for j in range(G):
                wait_alone(v, always, done, n.now() - (G - 1 - j))
                if j < G - 1:
                    V.bn_aggr(mv[:, j, :], stat[:, j, :])
                else:
                    V.bn_aggr(mv[:, j, :], stat[:, j, :]).then_inc(ready, 1)

        PER = 2 * G
        with v.Fori(0, NG) as i:
            n = Count(i, PER)
            for k, w in enumerate((weight1, weight2)):
                for j in range(G):
                    b = i * G + j
                    if k == 0:
                        v.wait_ge(s[f"y_in{j}"], (i + 1) * 32)
                    else:
                        v.wait_ge(done, n.now() - (G - 1 - j))
                    V.scalar_tensor_tensor(x_res[:, b, :], yg[:, j, k, :], w[:, bass.ds(b, 1)], x_res[:, b, :],
                                           ALU.mult, ALU.add).then_inc(done if k == 0 else s["mixed"], 1)
                    if k == 0:
                        n()
            wait_alone(v, always, s["mixed"], i * G + G)
            mean_var(lambda j: x_res[:, i * G + j, :], s["mv_ready"], n)
            v.wait_ge(s["mv_ready"], i + 1)
            v.wait_ge(s["rstd_ready"], i + 1)
            for j in range(G):
                V.tensor_scalar(xh[:, j, :], x_res[:, i * G + j, :], mv[:, j, 0:1], rstd[:, j:j + 1],
                                ALU.subtract, ALU.mult).then_inc(s["xh_ready"], 1)
            v.wait_ge(s["q1_ready"], i * C + C)
            for m in range(C):
                V.scalar_tensor_tensor(qr[:, m, :], bank[2 + m][:, 0:GS], 0.25, qa[:, 0, m, :], ALU.mult, ALU.subtract).then_inc(s["q_read"], 1)
            v.wait_ge(s["q_read"], i * C + C)
            V.tensor_copy(qa[:, 1, :, :], qr[:]).then_inc(s["q2_ready"], 1)
            v.wait_ge(s["q2_ready"], i + 1)
            V.tensor_tensor(qa[:, 2, :, :], qr[:], qa[:, 1, :, :], ALU.subtract).then_inc(s["q3_ready"], 1)
            assert n.n == PER

        def maximum(b, g, at):
            v.wait_ge(s["s_ps"], b * 8 + (g + 1))
            V.tensor_reduce(mxh[:, 2 * g:2 * g + 2], ps[0:S, 2 * (g % 2):2 * (g % 2) + 2, 0:K], axis=AX_X, op=ALU.max).then_inc(s["s_max"], 1)

        def negated_parts(b, slot):
            base = b * 4
            v.wait_ge(s["s_max"], b * 8 + 8)
            V.tensor_scalar(mparts[:, slot, 0, :], mxh[:], -1.0, None, ALU.mult).then_inc(s["m_ready"], 1)
            v.wait_ge(s["m_ready"], base + 1)
            V.scalar_tensor_tensor(mr[:, slot, :], mxh[:], -1.0, mparts[:, slot, 0, :], ALU.mult, ALU.subtract).then_inc(s["m_ready"], 1)
            v.wait_ge(s["m_ready"], base + 2)
            V.tensor_copy(mparts[:, slot, 1, :], mr[:, slot, :]).then_inc(s["m_ready"], 1)
            v.wait_ge(s["m_ready"], base + 3)
            V.tensor_tensor(mparts[:, slot, 2, :], mr[:, slot, :], mparts[:, slot, 1, :], ALU.subtract).then_inc(s["m_ready"], 1)
            v.wait_ge(s["mT_ps"], b + 1)

        def turned(b, slot):
            V.tensor_copy(mT[:, slot, :], ps[0:3 * NH, 0, 0:S // 2].bitcast(BF16)).then_inc(s["mT_ready"], 1)

        def first_pass(b, slot, free=None):
            for g in range(8):
                maximum(b, g, slot)
            negated_parts(b, slot)
            if free is not None:
                v.wait_ge(s[f"m_out{slot}"], free)
            turned(b, slot)

        def finish(b):
            v.wait_ge(s["pv_ps"], b + 1)
            out_ps = bank[7][0:S, 0:NH * (HD + 1)].rearrange("p (h d) -> p h d", d=HD + 1)
            V.reciprocal(rec[:].unsqueeze(2), out_ps[:, :, HD:HD + 1]).then_inc(s["heads_ready"], 1)
            v.wait_ge(s["heads_ready"], b * 2 + 1)
            V.tensor_tensor(heads[:, b, :].rearrange("p (h d) -> p h d", d=HD), out_ps[:, :, 0:HD],
                            rec[:].unsqueeze(2).to_broadcast([S, NH, HD]), ALU.mult).then_inc(s["heads_ready"], 1)

        first_pass(0, 0)
        first_pass(1, 1)

        def turn(i, last):
            for j in range(4):
                b = i * 4 + j
                if not last or j < 2:
                    first_pass(b + 2, j % 2, (i * 2 + (j // 2 + 1)) * 16)
                finish(b)

        with v.Fori(0, NG - 1) as i:
            turn(i, False)
        turn(NG - 1, True)

        def closing(i, first):
            n = Count(i, G, NG * PER)
            for j in range(G):
                v.wait_ge(s["o_ps"], i * G + (j + 1))
                V.tensor_tensor(x_res[:, i * G + j, :], bank[2 + j][0:S, 0:D], x_res[:, i * G + j, :], ALU.add).then_inc(s["x3_ready"], 1)
            wait_alone(v, always, s["x3_ready"], i * G + G)
            mean_var(lambda j: x_res[:, i * G + j, :], s["mv3_ready"], n)
            v.wait_ge(s["mv3_ready"], i + 1)
            v.wait_ge(s["rstd3_ready"], i + 1)
            for j in range(G):
                V.tensor_scalar(xh[:, j, :], x_res[:, i * G + j, :], mv[:, j, 0:1], rstd[:, j:j + 1],
                                ALU.subtract, ALU.mult).then_inc(s["xh3_ready"], 1)
            for j in range(G):
                v.wait_ge(s["f_ps"], i * G + (j + 1))
                if not first:
                    v.wait_ge(s[f"res_out{j}"], i * 16)
                V.tensor_tensor(res[:, j, :], bank[2 + j][0:S, 0:D], x_res[:, i * G + j, :], ALU.add).then_inc(s["res_ready"], 1)

        closing(0, True)
        with v.Fori(1, NG) as i:
            closing(i, False)

    @block.scalar
    def _(a):
        A = nc.scalar.activation
        def queries(i, first):
            for c in range(C):
                a.wait_ge(s["xhT_ps"], i * C + (c + 1))
                A(xhT[:, c, :], bank[c][:, 0:GS], ACT.Copy).then_inc(s["xhT_ready"], 1)
            for m in range(C):
                a.wait_ge(s["q_ps"], i * C + (m + 1))
                if m == 0 and not first:
                    a.wait_ge(s["q_out"], i * 32)
                A(qa[:, 0, m, :], bank[2 + m][:, 0:GS], ACT.Copy, scale=0.25).then_inc(s["q1_ready"], 1)

        queries(0, True)
        with a.Fori(1, NG) as i:
            queries(i, False)

        def exps(b, q):
            for k in range(NKC):
                a.wait_ge(s["st_ps"], (b * 4 + q) * NKC + (k + 1))
                A(pT[:, q % 2, k, :], bank[4 + k][0:KC, 0:QUAD * S], ACT.Exp).then_inc(s["p_ready"], 1)

        with a.Fori(0, B) as b:
            for q in range(4):
                exps(b, q)

        with a.Fori(0, NG) as i:
            wait_alone(a, always, s["heads_ready"], i * (2 * G) + 2 * G)
            A(xh[:], heads[:, bass.ds(i * G, G), :], ACT.Copy).then_inc(s["h_kept"], 1)
            for c in range(C):
                a.wait_ge(s["hT_ps"], i * C + (c + 1))
                A(xhT[:, c, :], bank[c][:, 0:GS], ACT.Copy).then_inc(s["hT_ready"], 1)
            for c in range(C):
                a.wait_ge(s["x3T_ps"], i * C + (c + 1))
                A(xhT[:, c, :], bank[c][:, 0:GS], ACT.Copy).then_inc(s["x3T_ready"], 1)

    @block.tensor
    def _(t):
        mm = nc.tensor.matmul

        def turn_over(src, sign):
            for c in range(C):
                for j in range(G):
                    last = nc.tensor.transpose(bank[c][:, j * S:(j + 1) * S], src[:, j, c * P:(c + 1) * P], ident[0:S, 0:S])
                last.then_inc(sign, 1)

        t.wait_ge(s["weights_in"], 16 * 6)
        for c in range(C):
            last = mm(bank[c][:, 0:D], vrT[:, c * P:(c + 1) * P], cfT[:], start=True, stop=True)
        last.then_inc(s["wf_ps"], 1)
        t.wait_ge(s["wf_ready"], 2)
        with t.Fori(0, NG) as i:
            t.wait_ge(s["xh_ready"], i * G + G)
            turn_over(xh, s["xhT_ps"])
            t.wait_ge(s["xhT_ready"], i * C + C)
            for m in range(C):
                for c in range(C):
                    last = mm(bank[2 + m][:, 0:GS], wq1[:, c, m * P:(m + 1) * P], xhT[:, c, :], start=c == 0, stop=c == C - 1)
                last.then_inc(s["q_ps"], 1)

        def scores(b, slot, g, free=True):
            if free:
                t.wait_ge(s["s_max"], b * 8 + (g - 1))
            for k in range(2):
                h = 2 * g + k
                last = mm(bank[2 * (g % 2) + k][0:S, 0:K], qst[0:DEPTH, slot, h, :], kst[0:DEPTH, slot, h, 0:K], start=True, stop=True)
            last.then_inc(s["s_ps"], 1)

        def maxima_T(b, slot):
            wait_alone(t, always, s["m_ready"], b * 4 + 4)
            nc.tensor.transpose(ps[0:3 * NH, 0, 0:S // 2].bitcast(BF16), mparts[:, slot % 2, :, :].rearrange("p s h -> p (s h)"),
                                identb[0:S, 0:S]).then_inc(s["mT_ps"], 1)

        def arrived(slot, count):
            t.wait_ge(s[f"k_in{slot}"], count * 6 * 16)
            t.wait_ge(s[f"qs_in{slot}"], count * 6 * 16)

        def transposed(b, slot, q, very_first):
            for k in range(NKC):
                if not very_first:
                    t.wait_ge(s["p_ready"], (b * 4 + (q - 1)) * NKC + (k + 1))
                for h in range(QUAD):
                    last = mm(bank[4 + k][0:KC, h * S:(h + 1) * S], kst[0:DEPTH + 3, slot, QUAD * q + h, k * KC:(k + 1) * KC],
                              qst[0:DEPTH + 3, slot, QUAD * q + h, :], start=True, stop=True)
                last.then_inc(s["st_ps"], 1)

        def outputs(b, slot, q):
            t.wait_ge(s["p_ready"], (b * 4 + q) * NKC + NKC)
            for h in range(QUAD):
                at = (QUAD * q + h) * (HD + 1)
                for k in range(NKC):
                    last = mm(bank[7][0:S, at:at + HD + 1], pT[:, q % 2, k, h * S:(h + 1) * S], vt[:, slot % 2, k, QUAD * q + h, :],
                              start=k == 0, stop=k == NKC - 1)
            if q == 3:
                last.then_inc(s["pv_ps"], 1)

        t.wait_ge(s["consts_ready"], 1)
        t.wait_ge(s["q3_ready"], NG)
        for b in range(2):
            arrived(b, 1)
            for g in range(8):
                if b and g == 0:
                    t.wait_ge(s["mT_ready"], b)
                scores(b, b, g, b or g >= 2)
            maxima_T(b, b)

        def second(b, i, j, very_first, last):
            ahead = not last or j < 2
            if ahead:
                arrived((j + 2) % 4, i + (1 if j < 2 else 2))
                t.wait_ge(s["mT_ready"], b + 2)
            t.wait_ge(s[f"mrow_in{j}"], (i + 1) * 16)
            t.wait_ge(s[f"v_in{j % 2}"], (i * 2 + (j // 2 + 1)) * 16)
            for q in range(4):
                if ahead:
                    for g in range(2 * q, 2 * q + 2):
                        scores(b + 2, (j + 2) % 4, g)
                transposed(b, j, q, very_first and q == 0)
                if q == 0 and not very_first:
                    outputs(b - 1, (j - 1) % 4, 3)
                if q == 1 and not very_first:
                    t.wait_ge(s["heads_ready"], b * 2)
                if q:
                    outputs(b, j, q - 1)
            if ahead:
                maxima_T(b + 2, j)

        for j in range(4):
            second(j, 0, j, j == 0, False)
        with t.Fori(1, NG - 1) as i:
            for j in range(4):
                second(i * 4 + j, i, j, False, False)
        for j in range(4):
            second((NG - 1) * 4 + j, NG - 1, j, False, True)
        outputs(B - 1, 3, 3)

        def closing(i, first):
            t.wait_ge(s["h_kept"], i + 1)
            turn_over(xh, s["hT_ps"])
            t.wait_ge(s["hT_ready"], i * C + C)
            for j in range(G):
                if not first:
                    t.wait_ge(s["res_ready"], (i - 1) * G + (j + 1))
                for c in range(C):
                    last = mm(bank[2 + j][0:S, 0:D], xhT[:, c, j * S:(j + 1) * S], wo1[:, c, :], start=c == 0, stop=c == C - 1)
                last.then_inc(s["o_ps"], 1)
            t.wait_ge(s["xh3_ready"], i * G + G)
            turn_over(xh, s["x3T_ps"])
            t.wait_ge(s["x3T_ready"], i * C + C)
            for j in range(G):
                for c in range(C):
                    mm(bank[2 + j][0:S, 0:D], xhT[:, c, j * S:(j + 1) * S], wf[:, c, :], start=c == 0, stop=False)
                last = mm(bank[2 + j][0:S, 0:D], ones[0:1, 0:S], bf_row[:], start=False, stop=True)
                last.then_inc(s["f_ps"], 1)

        closing(0, True)
        with t.Fori(1, NG) as i:
            closing(i, False)


def build_program(nc, dram, outs):
    ctx, semaphores = ExitStack(), ExitStack()
    with semaphores, ctx:
        def sb(name, shape, dt=F32):
            return ctx.enter_context(nc.sbuf_tensor(name, shape, dt))
        def sem(name):
            return ctx.enter_context(nc.semaphore(name))
        ps = ctx.enter_context(nc.psum_tensor("ps", [P, 8, 512], F32))
        bank = [ps[:, k, :] for k in range(8)]
        ident = sb("ident", [P, P])
        ones = sb("ones", [P, P])
        x_res = sb("x_res", [S, B, D])
        weight1 = sb("weight1", [S, B])
        weight2 = sb("weight2", [S, B])
        slots = sb("slots", [S, 2, B], I32)
        expert_row = sb("expert_row", [1, NTILE], I32)
        always = sem("always")
        nc.sync.sem_inc(always, 1)
        dram = dict(dram)
        for name, shape, dt in (
                ("xg", [NTILE * P, D], F32), ("yscr", [NTILE * P, D], F32), ("kscr", [B, 3, D, KP], BF16),
                ("vscr", [B, KC, NKC * NH * (HD + 1)], F32), ("qscr", [NG, 3, D, GS], BF16), ("mscr", [B, 3 * NH, S], BF16)):
            dram[name] = nc.dram_tensor(name, shape, dt, kind="Internal").ap()
        with ExitStack() as c_moe:
            xh_moe = c_moe.enter_context(nc.sbuf_tensor("xh_moe", [S, B, D], F32))
            logits = c_moe.enter_context(nc.sbuf_tensor("logits", [S, B, E], F32))
            with ExitStack() as given_on:
                with ExitStack() as c0:
                    names = layer0(nc, c0, dram, x_res, xh_moe, logits, bank, ident, ones, always, given_on)
                with nc.Block() as block:
                    @block.sync
                    def _(sp):
                        for name in names:
                            sp.sem_clear(name)
            weights = [c_moe.enter_context(nc.sbuf_tensor(f"rw{k}", shape, F32))
                       for k, shape in ((1, [P, E, C, H]), (2, [P, E, C, H]), (3, [P, E, HM, D]))]
            biases = [c_moe.enter_context(nc.sbuf_tensor(f"rb{k}", [P, E, n], F32)) for k, n in ((1, H), (2, H), (3, D))]
            with ExitStack() as c1:
                routing_and_projections(nc, c1, dram, xh_moe, logits, weight1, weight2, slots, expert_row,
                                        weights, biases, ps, bank, ones, always, semaphores)
            with ExitStack() as c2:
                routed_experts(nc, c2, dram, expert_row, weights, biases, ps, bank, ident, always, semaphores)
        with ExitStack() as c3:
            layer1(nc, c3, dram, outs["out"], x_res, weight1, weight2, slots, ps, bank, ident, ones, always, semaphores)


def lay_out(inputs):
    import numpy as np
    a = {k: np.asarray(v) for k, v in inputs.items()}
    t = lambda w: np.ascontiguousarray(w.T)
    x0, f0, x1, f1 = "L0_xattn_", "L0_ffn_", "L1_xattn_", "L1_ffn_"
    ctx_t = np.zeros((B, D, KP), np.float32)
    ctx_t[:, :, :K] = a["ctx_1024"].transpose(0, 2, 1)
    out = {
        "x": a["x"], "ctx": a["ctx_1024"], "ctx_t": ctx_t, "mask": a["mask_Bx1xS2_ik1"],
        "wq_t": t(a[x0 + "Wq"]), "wk_t": t(a[x0 + "Wk"]), "wv_t": t(a[x0 + "Wv"]), "wo0": a[x0 + "Wo"],
        "identity": np.eye(P, dtype=np.float32), "ones": np.ones((P, P), np.float32),
    }
    out["wk1_t"], out["wv1_t"], out["wq1_t"], out["wo1_t"] = (t(a[x1 + n]) for n in ("Wk", "Wv", "Wq", "Wo"))
    out["wf_t"], out["vr_t"], out["cf_t"], out["bf"] = t(a[f1 + "W"]), t(a[f1 + "V_r"]), t(a[f1 + "C"]), a[f1 + "b"]
    out["before"] = np.triu(np.ones((S, S), np.float32), 1)
    out["iota"] = np.tile(np.arange(E, dtype=np.float32), (S, 1))
    out["lower"] = np.tile(np.tril(np.ones((E, E), np.float32), -1), (S, 1, 1))
    out["steps"] = np.tile(P * np.arange(NT_E, dtype=np.float32), (S, 1))
    out["tiles"] = np.tile(np.arange(NTILE, dtype=np.float32), (S, 1))
    out["qkv_bias"] = np.stack([a[x0 + n].reshape(C, P).T for n in ("bq", "bk", "bv")], 1)
    out["sb12"] = np.stack([a[f0 + n].reshape(SE * HM, P).T for n in ("sb1", "sb2")], 1)
    for n in ("bo", "g0", "beta0"):
        out[n] = a[x0 + n]
    for n in ("gate_w", "gate_b", "sw1", "sw2", "sw3", "sb3", "rw1", "rb1", "rw2", "rb2", "rw3", "rb3"):
        out[n] = a[f0 + n]
    return {k: np.ascontiguousarray(v) for k, v in out.items()}


def kernel(**inputs):
    import concourse.bacc as bacc
    import numpy as np
    from concourse.bass_utils import run_bass_kernel_spmd

    nc = bacc.Bacc("TRN2", target_bir_lowering=False, num_devices=1)
    arrays = {f"in_{name}": a for name, a in lay_out(inputs).items()}
    dram = {name[3:]: nc.dram_tensor(name, a.shape, mybir.dt.from_np(a.dtype), kind="ExternalInput").ap()
            for name, a in arrays.items()}
    outs = {"out": nc.dram_tensor("out", (B, S, D), F32, kind="ExternalOutput").ap()}
    build_program(nc, dram, outs)
    got = run_bass_kernel_spmd(nc, [arrays], core_ids=[0])
    return got.results[0]["out"]
```

```python
from contextlib import ExitStack

import concourse.bass as bass
from concourse import mybir

F32 = mybir.dt.float32
BF16 = mybir.dt.bfloat16
I32 = mybir.dt.int32
ALU = mybir.AluOpType
AX_X = mybir.AxisListType.X
ACT = mybir.ActivationFunctionType

P = 128
B, S, D = 16, 112, 256
K = 375
KC = 125
NKC = K // KC
KP = (NKC - 1) * KC + P
C = D // P
G = 4
NG = B // G
GS = G * S
E, SE, H = 8, 2, 512
HM = H // P
NH, HD = 16, 16
NT_E = B * S // P
NTILE = 2 * B * S // P + E
EPS = 1e-5
NEG = -1e9


class Count:

    def __init__(self, turn=0, per=0, base=0):
        self.turn, self.per, self.base, self.n = turn, per, base, 0

    def __call__(self, n=1):
        self.n += n
        return self.now()

    def now(self):
        return self.turn * self.per + (self.base + self.n)


def wait_alone(eng, always, semaphore, value):
    value = eng.to_reg(value)
    eng.wait_ge(always, 1)
    eng.wait_ge(semaphore, value)


def layer0(nc, ctx, dram, x_res, xh_moe, logits, rw1, bank, ident, ones, always, new_semaphore):

    def sb(name, shape, dt=F32):
        return ctx.enter_context(nc.sbuf_tensor(name, shape, dt))

    def sem(name):
        return new_semaphore(name)

    wqk = sb("wqk", [P, C, D])
    wvo = sb("wvo", [P, C, D])
    cols = sb("cols", [P, 3, C])
    bqk = sb("bqk", [P, C])
    wqbk = sb("wqbk", [P, C])
    rep = sb("rep", [P, 2, C, S])
    cb = sb("cb", [S, 1])
    bo_row = sb("bo_row", [1, D])
    bo_b = sb("bo_b", [S, D])
    g0_b = sb("g0_b", [S, D])
    beta_b = sb("beta_b", [S, D])
    gw = sb("gw", [P, C, E])
    gb_row = sb("gb_row", [1, E])
    sw1 = sb("sw1", [P, SE, C, H])
    sw2 = sb("sw2", [P, SE, C, H])
    sw3 = sb("sw3", [P, SE, HM, D])
    sb12 = sb("sb12", [P, 2, SE * HM])
    sb3_rows = sb("sb3_rows", [1, SE, D])
    stat = sb("stat", [S, G, 6])
    mv = sb("mv", [S, G, 2])
    rstd = sb("rstd", [S, G])
    mhalf = sb("mhalf", [S, G])
    xh = sb("xh", [S, G, D])
    xhT = sb("xhT", [P, C, GS])
    qT = sb("qT", [P, C, GS])
    cq = sb("cq", [S, G])
    ctxT = sb("ctxT", [P, G, C, KP])
    ctxn = sb("ctxn", [KC, G, NKC, D])
    mask_i = sb("mask_i", [S, G, K], I32)
    drop = sb("drop", [S, G, K])
    keep = sb("keep", [S, G, K])
    add = drop
    sc = sb("sc", [S, 2, K])
    scm = sb("scm", [S, 2, K])
    mx = sb("mx", [S, G])
    nmx = sb("nmx", [S, G])
    probs = sb("probs", [S, 2, K])
    rsum = sb("rsum", [S, G])
    rrec = sb("rrec", [S, G])
    pT = sb("pT", [KC, 2, NKC * S])
    uT = sb("uT", [P, 2, C * S])
    o_sb = sb("o_sb", [S, G, D])
    silu = sb("silu", [P, 2, GS])
    gluT = sb("gluT", [P, SE * HM, GS])
    given = gluT[:].rearrange("p m t -> p (m t)")
    wq_t, wk_t, wv_t, wo = (given[:, k * C * D:(k + 1) * C * D].rearrange("p (c n) -> p c n", c=C) for k in range(4))
    zeros = sb("zeros", [P, D])
    wv1 = sb("wv1", [P, C, D])
    va = sb("va", [KC, G, NKC, NH, HD + 1])

    s = {n: sem(n) for n in (
        "shared_in", "x_in", "others_in", "rw1_in", "v_out0", "v_out1", "v_out2", "v_out3", "weights_in", "consts_in", "zeroed", "fold_ps", "folded", "ctx_in0", "ctx_in1", "ctx_in2", "ctx_in3", "mask_in0", "mask_in1", "mask_in2", "mask_in3",
        "dve0", "pool0", "mv_ready", "rstd_ready", "xh_ready", "xhT_ps", "xhT_ready", "q_ps",
        "q_ready", "c_ps", "s_ps", "s_read", "keep_ready", "max_ready", "p_ready", "pT_ps", "pT_ready",
        "u_ps", "uT_ready", "o_ps", "o_read", "mv1_ready", "rstd1_ready", "mv2_ready", "rstd2_ready",
        "xh1_ready", "xh1T_ps", "xh1T_ready", "gate_ps", "gate_read", "p12_ps", "silu_ready",
        "glu_ready", "sh_ps", "sh_read", "v_ps", "v_ready", "kept", "xh_kept", "consts_ready", "zeros_ready")}
    ctx_in = [s[f"ctx_in{j}"] for j in range(G)]
    psum_T = bank[0:2]
    psum_q = bank[2:4]
    psum_s = bank[4:6]
    psum_pT, psum_u = bank[6], bank[7]

    block = ctx.enter_context(nc.Block())

    @block.sync
    def _(sp):
        for dst, name in ((wq_t, "wq_t"), (wk_t, "wk_t"), (wv_t, "wv_t"), (wo, "wo0")):
            sp.dma_start(dst, dram[name].rearrange("(c p) n -> p c n", p=P)).then_inc(s["weights_in"], 16)
        sp.dma_start(cols[:], dram["qkv_bias"]).then_inc(s["weights_in"], 16)
        sp.dma_start(bo_row[:], dram["bo"].rearrange("(o n) -> o n", o=1)).then_inc(s["weights_in"], 16)
        sp.dma_start(x_res[:], dram["x"].rearrange("b s d -> s b d")).then_inc(s["x_in"], 16)
        for dst, name in ((g0_b, "g0"), (beta_b, "beta0")):
            sp.dma_start(dst[:], dram[name].rearrange("(o n) -> o n", o=1).to_broadcast([S, D])).then_inc(s["others_in"], 16)
        sp.dma_start(gw[:], dram["gate_w"].rearrange("(c p) n -> p c n", p=P)).then_inc(s["others_in"], 16)
        sp.dma_start(gb_row[:], dram["gate_b"].rearrange("(o n) -> o n", o=1)).then_inc(s["others_in"], 16)
        sp.dma_start(sb12[:], dram["sb12"]).then_inc(s["others_in"], 16)
        sp.dma_start(sb3_rows[:], dram["sb3"].rearrange("(o e) n -> o e n", o=1)).then_inc(s["others_in"], 16)
        sp.dma_start(wv1[:], dram["wv1_t"].rearrange("(c p) n -> p c n", p=P)).then_inc(s["others_in"], 16)

        def load_context(b, j):
            sp.dma_start(ctxT[:, j, :, :], dram["ctx_t"][b].rearrange("(c p) k -> p c k", p=P)).then_inc(ctx_in[j], 16)
            sp.dma_start(ctxn[:, j, :, :], dram["ctx"][b].rearrange("(c p) d -> p c d", p=KC)).then_inc(ctx_in[j], 16)

        def store_values(i, j):
            sp.wait_ge(s["v_ready"], i * G + (j + 1))
            sp.dma_start(dram["vscr"][i * G + j], va[:, j, :, :, :].rearrange("p c h d -> p (c h d)")).then_inc(s[f"v_out{j}"], 16)

        def load_mask(b, j):
            sp.dma_start(mask_i[:, j, :], dram["mask"][b].to_broadcast([S, K])).then_inc(s[f"mask_in{j}"], 16)

        def load_experts(i):
            for k in range(E // NG):
                e = i * (E // NG) + k
                sp.dma_start(rw1[:, bass.ds(e, 1), :, :].rearrange("p e c n -> p (e c) n"),
                             dram["rw1"][bass.ds(e, 1), :, :].rearrange("e (c p) n -> p (e c) n", p=P)).then_inc(s["rw1_in"], 16)

        for j in range(G):
            load_context(j, j)
            load_mask(j, j)
        sp.wait_ge(s["zeros_ready"], 1)
        sp.dma_start(dram["xg"].rearrange("(p r) d -> p r d", p=P), zeros[:].unsqueeze(1).to_broadcast([P, NTILE, D])).then_inc(s["zeroed"], 16)
        load_experts(0)
        with sp.Fori(1, NG) as i:
            for j in range(G):
                if j < 2:
                    store_values(i - 1, j)
                sp.wait_ge(s["u_ps"], (i - 1) * G + (j + 1))
                if j >= 2:
                    sp.wait_ge(s["v_ps"], (i - 1) * G + (j + 1))
                load_context(i * G + j, j)
                sp.wait_ge(s["keep_ready"], (i - 1) * G + (j + 1))
                load_mask(i * G + j, j)
                if j >= 2:
                    store_values(i - 1, j)
            load_experts(i)
        for j in range(G):
            store_values(NG - 1, j)
        sp.wait_ge(s["rw1_in"], 16 * E)
        sp.wait_ge(s["zeroed"], 16)
        for j in range(G):
            sp.wait_ge(s[f"v_out{j}"], 16 * NG)

    @block.gpsimd
    def _(pool):
        for dst, name in ((sw1, "sw1"), (sw2, "sw2"), (sw3, "sw3")):
            pool.dma_start(dst[:], dram[name].rearrange("e (c p) n -> p e c n", p=P)).then_inc(s["shared_in"], 16)
        pool.memset(zeros[:], 0.0).then_inc(s["zeros_ready"], 1)
        pool.memset(va[:], 1.0).then_inc(s["zeros_ready"], 1)
        pool.memset(mhalf[:], -0.5).then_inc(s["pool0"], 1)
        pool.wait_ge(s["pool0"], 1)
        pool.sem_inc(s["xh_kept"], 1)
        pc = 1

        def power(pool, mean_var, ready, n, done, pbase):
            wait_alone(pool, always, ready, n)
            pool.tensor_scalar(rstd[:], mean_var[:, :, 1], EPS, None, ALU.add).then_inc(s["pool0"], 1)
            wait_alone(pool, always, s["pool0"], pbase)
            pool.tensor_tensor(rstd[:], rstd[:], mhalf[:], ALU.pow).then_inc(done, 1)

        with pool.Fori(0, NG) as i:
            per = 3 + G
            power(pool, mv, s["mv_ready"], i + 1, s["rstd_ready"], i * per + (pc + 1))
            for j in range(G):
                wait_alone(pool, always, s[f"mask_in{j}"], (i + 1) * 16)
                if j == 0:
                    wait_alone(pool, always, s["max_ready"], i * G + G)
                pool.tensor_scalar(drop[:, j, :], mask_i[:, j, :], 0.0, None, ALU.is_equal).then_inc(s["pool0"], 1)
                wait_alone(pool, always, s["pool0"], i * per + (pc + 2 + j))
                pool.tensor_scalar(keep[:, j, :], drop[:, j, :], -1.0, 1.0, ALU.mult, ALU.add).then_inc(s["kept"], 1)
                wait_alone(pool, always, s["kept"], i * G + (j + 1))
                pool.tensor_scalar(add[:, j, :], drop[:, j, :], NEG, None, ALU.mult).then_inc(s["keep_ready"], 1)
            power(pool, mv, s["mv1_ready"], i + 1, s["rstd1_ready"], i * per + (pc + 2 + G))
            power(pool, mv, s["mv2_ready"], i + 1, s["rstd2_ready"], i * per + (pc + 3 + G))
            wait_alone(pool, always, s["xh1_ready"], i * G + G)
            pool.tensor_copy(xh_moe[:, bass.ds(i * G, G), :], xh[:]).then_inc(s["xh_kept"], 1)

    @block.vector
    def _(v):
        done = s["dve0"]
        v.sem_inc(s["max_ready"], G)
        v.wait_ge(s["weights_in"], 16 * 6)
        v.wait_ge(s["consts_in"], 32)
        for k in range(2):
            for c in range(C):
                nc.vector.tensor_scalar(rep[:, k, c, :], ones[:, 0:S], cols[:, 2 * k, c:c + 1], None, ALU.mult).then_inc(done, 1)
        v.wait_ge(done, 4)
        v.sem_inc(s["consts_ready"], 1)
        v.wait_ge(s["fold_ps"], 1)
        for c in range(C):
            nc.vector.tensor_scalar(wqk[:, c, :], bank[c][:, 0:D], 1.0 / 16, None, ALU.mult)
            nc.vector.tensor_copy(wvo[:, c, :], bank[2 + c][:, 0:D])
        nc.vector.tensor_scalar(bqk[:], bank[4][:, 0:C], 1.0 / 16, None, ALU.mult)
        nc.vector.tensor_scalar(wqbk[:], bank[4][:, C:2 * C], 1.0 / 16, None, ALU.mult)
        nc.vector.tensor_scalar(cb[:], bank[5][0:S, 0:1], 1.0 / 16, None, ALU.mult)
        nc.vector.tensor_copy(bo_b[:], bank[6][0:S, 0:D]).then_inc(s["folded"], 1)
        v.wait_ge(s["folded"], 1)
        v.wait_ge(s["others_in"], 16 * 7)
        v.wait_ge(s["x_in"], 16)
        PER = 8 * G + 1
        with v.Fori(0, NG) as i:
            n = Count(i, PER, 4)

            def mean_var(src, ready, extra_wait=None):
                for j in range(G):
                    nc.vector.bn_stats(stat[:, j, :], src(j)).then_inc(done, 1)
                    n()
                for j in range(G):
                    wait_alone(v, always, done, n.now() - (G - 1 - j))
                    if j < G - 1:
                        nc.vector.bn_aggr(mv[:, j, :], stat[:, j, :])
                    else:
                        nc.vector.bn_aggr(mv[:, j, :], stat[:, j, :]).then_inc(ready, 1)

            mean_var(lambda j: x_res[:, i * G + j, :], s["mv_ready"])
            v.wait_ge(s["mv_ready"], i + 1)
            v.wait_ge(s["rstd_ready"], i + 1)
            v.wait_ge(s["xh_kept"], i + 1)
            for j in range(G):
                nc.vector.tensor_scalar(xh[:, j, :], x_res[:, i * G + j, :], mv[:, j, 0:1], rstd[:, j:j + 1],
                                        ALU.subtract, ALU.mult).then_inc(s["xh_ready"], 1)
            v.wait_ge(s["c_ps"], i + 1)
            nc.vector.tensor_scalar(cq[:], bank[1][0:S, GS:GS + G], cb[:, 0:1], None, ALU.add).then_inc(done, 1)
            n()
            v.wait_ge(done, n.now())

            def scores(j):
                v.wait_ge(s["s_ps"], i * G + (j + 1))
                v.wait_ge(s["keep_ready"], i * G + (j + 1))
                if j >= 2:
                    v.wait_ge(s["p_ready"], i * G + (j - 1))
                nc.vector.scalar_tensor_tensor(sc[:, j % 2, :], psum_s[j % 2][0:S, 0:K], cq[:, j:j + 1],
                                               keep[:, j, :], ALU.add, ALU.mult).then_inc(s["s_read"], 1)
                wait_alone(v, always, s["s_read"], i * G + (j + 1))
                nc.vector.tensor_tensor_reduce(out=scm[:, j % 2, :], in0=sc[:, j % 2, :], in1=add[:, j, :], scale=1.0,
                                               scalar=-3e38, op0=ALU.add, op1=ALU.max,
                                               accum_out=mx[:, j:j + 1]).then_inc(done, 1)
                n()
                v.wait_ge(done, n.now())
                nc.vector.tensor_scalar(nmx[:, j:j + 1], mx[:, j:j + 1], -1.0, None, ALU.mult).then_inc(s["max_ready"], 1)

            def u_out(j):
                v.wait_ge(s["u_ps"], i * G + (j + 1))
                nc.vector.tensor_copy(uT[:, j % 2, :], psum_u[:, 0:C * S]).then_inc(s["uT_ready"], 1)

            def o_out(j):
                v.wait_ge(s["p_ready"], i * G + (j + 1))
                nc.vector.reciprocal(rrec[:, j:j + 1], rsum[:, j:j + 1]).then_inc(done, 1)
                n()
                v.wait_ge(done, n.now())
                v.wait_ge(s["o_ps"], i * G + (j + 1))
                nc.vector.scalar_tensor_tensor(o_sb[:, j, :], psum_T[j % 2][0:S, 0:D], rrec[:, j:j + 1], bo_b[:],
                                               ALU.mult, ALU.add).then_inc(s["o_read"], 1)

            scores(0)
            scores(1)
            scores(2)
            u_out(0)
            scores(3)
            o_out(0)
            for j in range(1, G):
                u_out(j)
                o_out(j)
            wait_alone(v, always, s["o_read"], i * G + G)
            mean_var(lambda j: o_sb[:, j, :], s["mv1_ready"])
            v.wait_ge(s["mv1_ready"], i + 1)
            v.wait_ge(s["rstd1_ready"], i + 1)
            for step in range(3):
                for j in range(G):
                    if step == 0:
                        nc.vector.scalar_tensor_tensor(o_sb[:, j, :], o_sb[:, j, :], mv[:, j, 0:1], g0_b[:],
                                                       ALU.subtract, ALU.mult).then_inc(done, 1)
                    elif step == 1:
                        v.wait_ge(done, n.now() - (G - 1))
                        nc.vector.scalar_tensor_tensor(o_sb[:, j, :], o_sb[:, j, :], rstd[:, j:j + 1], beta_b[:],
                                                       ALU.mult, ALU.add).then_inc(done, 1)
                    else:
                        v.wait_ge(done, n.now() - (G - 1))
                        nc.vector.tensor_tensor(x_res[:, i * G + j, :], x_res[:, i * G + j, :], o_sb[:, j, :],
                                                ALU.add).then_inc(done, 1)
                    n()
            wait_alone(v, always, done, n.now())
            mean_var(lambda j: x_res[:, i * G + j, :], s["mv2_ready"])
            v.wait_ge(s["mv2_ready"], i + 1)
            v.wait_ge(s["rstd2_ready"], i + 1)
            for j in range(G):
                nc.vector.tensor_scalar(xh[:, j, :], x_res[:, i * G + j, :], mv[:, j, 0:1], rstd[:, j:j + 1],
                                        ALU.subtract, ALU.mult).then_inc(s["xh1_ready"], 1)
            v.wait_ge(s["gate_ps"], i + 1)
            nc.vector.tensor_copy(logits[:, bass.ds(i * G, G), :], bank[6][0:S, 0:G * E].rearrange("p (g e) -> p g e", g=G)).then_inc(s["gate_read"], 1)
            for m in range(SE * HM):
                v.wait_ge(s["silu_ready"], i * (SE * HM) + (m + 1))
                nc.vector.scalar_tensor_tensor(gluT[:, m, :], bank[3 + 2 * (m % 2)][:, 0:GS], sb12[:, 1, m:m + 1],
                                               silu[:, m % 2, :], ALU.add, ALU.mult).then_inc(s["glu_ready"], 1)
            for j in range(G):
                v.wait_ge(s["sh_ps"], i * G + (j + 1))
                nc.vector.scalar_tensor_tensor(x_res[:, i * G + j, :], bank[7 - j % 2][0:S, 0:D], 1.0 / SE,
                                               x_res[:, i * G + j, :], ALU.mult, ALU.add).then_inc(s["sh_read"], 1)
            assert n.n == PER

    @block.scalar
    def _(a):
        a.dma_start(ident[:], dram["identity"]).then_inc(s["consts_in"], 16)
        a.dma_start(ones[:], dram["ones"]).then_inc(s["consts_in"], 16)
        a.wait_ge(s["zeros_ready"], 2)
        a.wait_ge(s["folded"], 1)
        a.wait_ge(s["others_in"], 16 * 7)

        def values(i, j, first):
            a.wait_ge(s["v_ps"], i * G + (j + 1))
            if not first:
                a.wait_ge(s[f"v_out{j}"], i * 16)
            nc.scalar.activation(va[:, j, 0:2, :, 0:HD],
                                 bank[2 + 2 * (j % 2)][0:KC, :].rearrange("p (c h d) -> p c h d", c=2, d=HD), ACT.Copy)
            nc.scalar.activation(va[:, j, 2, :, 0:HD],
                                 bank[3 + 2 * (j % 2)][0:KC, 0:D].rearrange("p (h d) -> p h d", d=HD), ACT.Copy).then_inc(s["v_ready"], 1)

        def group(i, first):
            for j in range(2):
                values(i, j, first)
            for c in range(C):
                a.wait_ge(s["xhT_ps"], i * C + (c + 1))
                nc.scalar.activation(xhT[:, c, :], psum_T[c][:, 0:GS], ACT.Identity).then_inc(s["xhT_ready"], 1)
            for m in range(C):
                a.wait_ge(s["q_ps"], i * C + (m + 1))
                nc.scalar.activation(qT[:, m, :], psum_q[m][:, 0:GS], ACT.Identity, bias=bqk[:, m:m + 1]).then_inc(s["q_ready"], 1)

            def exps(j):
                a.wait_ge(s["max_ready"], i * G + (j + 1 + G))
                nc.scalar.activation(probs[:, j % 2, :], scm[:, j % 2, :], ACT.Exp, bias=nmx[:, j:j + 1],
                                     accum_out=rsum[:, j:j + 1]).then_inc(s["p_ready"], 1)

            def p_out(j):
                a.wait_ge(s["pT_ps"], i * G + (j + 1))
                if j >= 2:
                    a.wait_ge(s["u_ps"], i * G + (j - 1))
                nc.scalar.activation(pT[:, j % 2, :], psum_pT[0:KC, 0:NKC * S], ACT.Identity).then_inc(s["pT_ready"], 1)

            exps(0)
            exps(1)
            for j in range(G):
                p_out(j)
                if j + 2 < G:
                    exps(j + 2)
            for j in range(2, G):
                values(i, j, first)
            for c in range(C):
                a.wait_ge(s["xh1T_ps"], i * C + (c + 1))
                nc.scalar.activation(xhT[:, c, :], psum_T[c][:, 0:GS], ACT.Identity).then_inc(s["xh1T_ready"], 1)
            for m in range(SE * HM):
                a.wait_ge(s["p12_ps"], i * (SE * HM) + (m + 1))
                if m >= 2:
                    a.wait_ge(s["glu_ready"], i * (SE * HM) + (m - 1))
                nc.scalar.activation(silu[:, m % 2, :], bank[2 + 2 * (m % 2)][:, 0:GS], ACT.Silu,
                                     bias=sb12[:, 0, m:m + 1]).then_inc(s["silu_ready"], 1)

        group(0, True)
        with a.Fori(1, NG) as i:
            group(i, False)

    @block.tensor
    def _(t):
        mm = nc.tensor.matmul
        t.wait_ge(s["weights_in"], 16 * 6)
        t.wait_ge(s["consts_in"], 32)
        t.wait_ge(s["consts_ready"], 1)
        for c in range(C):
            for k in range(C):
                mm(bank[c][:, 0:D], wq_t[:, k, c * P:(c + 1) * P], wk_t[:, k, :], start=k == 0, stop=k == C - 1)
            for k in range(C):
                mm(bank[2 + c][:, 0:D], wv_t[:, k, c * P:(c + 1) * P], wo[:, k, :], start=k == 0, stop=k == C - 1)
        for c in range(C):
            for k in range(C):
                mm(bank[4][:, c:c + 1], wk_t[:, k, c * P:(c + 1) * P], cols[:, 0, k:k + 1], start=k == 0, stop=k == C - 1)
        for c in range(C):
            for k in range(C):
                mm(bank[4][:, C + c:C + c + 1], wq_t[:, k, c * P:(c + 1) * P], cols[:, 1, k:k + 1], start=k == 0, stop=k == C - 1)
        for k in range(C):
            mm(bank[5][0:S, 0:1], rep[:, 0, k, :], cols[:, 1, k:k + 1], start=k == 0, stop=k == C - 1)
        for k in range(C):
            mm(bank[6][0:S, 0:D], rep[:, 1, k, :], wo[:, k, :], start=k == 0, stop=False)
        mm(bank[6][0:S, 0:D], ones[0:1, 0:S], bo_row[:], start=False, stop=True).then_inc(s["fold_ps"], 1)
        t.wait_ge(s["folded"], 1)
        t.wait_ge(s["others_in"], 16 * 7)
        with t.Fori(0, NG) as i:
            def values(j):
                t.wait_ge(ctx_in[j], (i + 1) * 32)
                if j >= 2:
                    t.wait_ge(s["v_ready"], i * G + (j - 1))
                for k in range(NKC):
                    for c in range(C):
                        last = mm(bank[2 + 2 * (j % 2) + k // 2][0:KC, (k % 2) * D:(k % 2 + 1) * D], ctxT[:, j, c, k * KC:(k + 1) * KC],
                                  wv1[:, c, :], start=c == 0, stop=c == C - 1)
                last.then_inc(s["v_ps"], 1)

            values(0)
            values(1)
            t.wait_ge(s["xh_ready"], i * G + G)
            for c in range(C):
                for j in range(G):
                    last = nc.tensor.transpose(psum_T[c][:, j * S:(j + 1) * S], xh[:, j, c * P:(c + 1) * P], ident[0:S, 0:S])
                last.then_inc(s["xhT_ps"], 1)
            t.wait_ge(s["xhT_ready"], i * C + C)
            t.wait_ge(s["v_ready"], i * G + 2)
            for m in range(C):
                for c in range(C):
                    last = mm(psum_q[m][:, 0:GS], wqk[:, c, m * P:(m + 1) * P], xhT[:, c, :], start=c == 0, stop=c == C - 1)
                last.then_inc(s["q_ps"], 1)
            for j in range(G):
                for c in range(C):
                    last = mm(psum_T[1][0:S, GS + j:GS + j + 1], xhT[:, c, j * S:(j + 1) * S], wqbk[:, c:c + 1], start=c == 0, stop=c == C - 1)
            last.then_inc(s["c_ps"], 1)
            t.wait_ge(s["q_ready"], i * C + C)

            def scores(j):
                t.wait_ge(ctx_in[j], (i + 1) * 32)
                if j >= 2:
                    t.wait_ge(s["s_read"], i * G + (j - 1))
                for c in range(C):
                    last = mm(psum_s[j % 2][0:S, 0:K], qT[:, c, j * S:(j + 1) * S], ctxT[:, j, c, 0:K], start=c == 0, stop=c == C - 1)
                last.then_inc(s["s_ps"], 1)

            def p_T(j):
                t.wait_ge(s["p_ready"], i * G + (j + 1))
                for k in range(NKC):
                    last = nc.tensor.transpose(psum_pT[0:KC, k * S:(k + 1) * S], probs[:, j % 2, k * KC:(k + 1) * KC], ident[0:S, 0:S])
                last.then_inc(s["pT_ps"], 1)

            def u(j):
                t.wait_ge(s["pT_ready"], i * G + (j + 1))
                for m in range(C):
                    for k in range(NKC):
                        last = mm(psum_u[:, m * S:(m + 1) * S], ctxn[:, j, k, m * P:(m + 1) * P], pT[:, j % 2, k * S:(k + 1) * S],
                                  start=k == 0, stop=k == NKC - 1)
                last.then_inc(s["u_ps"], 1)

            def o(j):
                t.wait_ge(s["uT_ready"], i * G + (j + 1))
                if j >= 2:
                    t.wait_ge(s["o_read"], i * G + (j - 1))
                for c in range(C):
                    last = mm(psum_T[j % 2][0:S, 0:D], uT[:, j % 2, c * S:(c + 1) * S], wvo[:, c, :], start=c == 0, stop=c == C - 1)
                last.then_inc(s["o_ps"], 1)

            scores(0)
            scores(1)
            p_T(0)
            scores(2)
            u(0)
            p_T(1)
            o(0)
            scores(3)
            for j in range(1, G):
                u(j)
                if j + 1 < G:
                    p_T(j + 1)
                o(j)
            values(2)
            values(3)
            t.wait_ge(s["xh1_ready"], i * G + G)
            for c in range(C):
                for j in range(G):
                    last = nc.tensor.transpose(psum_T[c][:, j * S:(j + 1) * S], xh[:, j, c * P:(c + 1) * P], ident[0:S, 0:S])
                last.then_inc(s["xh1T_ps"], 1)
            t.wait_ge(s["xh1T_ready"], i * C + C)
            for j in range(G):
                for c in range(C):
                    mm(bank[6][0:S, j * E:(j + 1) * E], xhT[:, c, j * S:(j + 1) * S], gw[:, c, :], start=c == 0, stop=False)
                last = mm(bank[6][0:S, j * E:(j + 1) * E], ones[0:1, 0:S], gb_row[:], start=False, stop=True)
            last.then_inc(s["gate_ps"], 1)
            t.wait_ge(s["shared_in"], 48)
            t.wait_ge(s["v_ready"], i * G + G)
            for m in range(SE * HM):
                e, h = divmod(m, HM)
                if m >= 2:
                    t.wait_ge(s["glu_ready"], i * (SE * HM) + (m - 1))
                for k, w in enumerate((sw1, sw2)):
                    for c in range(C):
                        last = mm(bank[2 + 2 * (m % 2) + k][:, 0:GS], w[:, e, c, h * P:(h + 1) * P], xhT[:, c, :], start=c == 0, stop=c == C - 1)
                last.then_inc(s["p12_ps"], 1)
            t.wait_ge(s["glu_ready"], i * (SE * HM) + SE * HM)
            t.wait_ge(s["gate_read"], i + 1)
            for j in range(G):
                if j >= 2:
                    t.wait_ge(s["sh_read"], i * G + (j - 1))
                for m in range(SE * HM):
                    e, h = divmod(m, HM)
                    mm(bank[7 - j % 2][0:S, 0:D], gluT[:, m, j * S:(j + 1) * S], sw3[:, e, h, :], start=m == 0, stop=False)
                for e in range(SE):
                    last = mm(bank[7 - j % 2][0:S, 0:D], ones[0:1, 0:S], sb3_rows[:, e, :], start=False, stop=e == SE - 1)
                last.then_inc(s["sh_ps"], 1)


def routing_and_projections(nc, ctx, dram, xh_moe, logits, weight1, weight2, slots, expert_row,
                            weights, biases, ps, bank, ones, always, new_semaphore):

    def sb(name, shape, dt=F32):
        return ctx.enter_context(nc.sbuf_tensor(name, shape, dt))

    def sem(name):
        return new_semaphore(name)

    TE = B * E
    before = sb("before", [S, S])
    iota = sb("iota", [S, E])
    lower = sb("lower", [S, E, E])
    steps = sb("steps", [S, NT_E])
    tiles = sb("tiles", [S, NTILE])
    top = sb("top", [S, B])
    gates = sb("gates", [S, B, E])
    hit = sb("hit", [S, B, E])
    cand = sb("cand", [S, B, E])
    index = sb("index", [S, B])
    one1 = sb("one1", [S, B, E])
    one2 = sb("one2", [S, B, E])
    both = sb("both", [S, 2 * B, E])
    count = sb("count", [S, E])
    over = sb("over", [S, E, NT_E])
    ntile = sb("ntile", [S, E])
    prod = sb("prod", [S, E, E])
    first = sb("first", [S, E])
    first128 = sb("first128", [S, E])
    slot = gates
    slot_f = sb("slot_f", [S, 2, B])
    started = sb("started", [S, E - 1, NTILE])
    expert_f = sb("expert_f", [S, NTILE])
    wk1 = sb("wk1", [P, C, D])
    cT = sb("cT", [P, 4, C, KP])
    ka = sb("ka", [P, 2, 3, C, KP], BF16)
    kr = sb("kr", [P, 2, C, KP])

    s = {n: sem("b_" + n) for n in (
        "consts_in", "weights_in", "ctx_in0", "ctx_in1", "dve", "sub_ready", "exp_ready", "both_ready",
        "pos_ps", "slots_ready", "scattered", "k_ps", "k_read", "k1_ready", "k2_ready", "k3_ready",
        "ctx_in2", "ctx_in3", "k_out0", "k_out1", "experts_in")}
    block = ctx.enter_context(nc.Block())
    kscr, xg = dram["kscr"], dram["xg"]

    @block.sync
    def _(sp):
        sp.dma_start(wk1[:], dram["wk1_t"].rearrange("(c p) n -> p c n", p=P)).then_inc(s["weights_in"], 16)
        for dst, name in ((before, "before"), (iota, "iota"), (lower, "lower"), (steps, "steps"), (tiles, "tiles")):
            sp.dma_start(dst[:], dram[name]).then_inc(s["consts_in"], 16)

        def load_context(b, q):
            sp.dma_start(cT[:, q, :, :], dram["ctx_t"][b].rearrange("(c p) k -> p c k", p=P)).then_inc(s[f"ctx_in{q}"], 16)

        for q in range(4):
            load_context(q, q)

        def store_keys(b, q):
            sp.wait_ge(s["k3_ready"], b + 1)
            for m in range(C):
                sp.dma_start(kscr[b][:, m * P:(m + 1) * P, :].rearrange("s f k -> f s k"), ka[:, q % 2, :, m, :]).then_inc(s[f"k_out{q % 2}"], 16)

        with sp.Fori(0, B // 4 - 1) as i:
            for q in range(4):
                store_keys(i * 4 + q, q)
                load_context(i * 4 + (q + 4), q)
        for q in range(4):
            store_keys(B - 4 + q, q)
        for q in range(2):
            sp.wait_ge(s[f"k_out{q}"], 32 * (B // 2))

    @block.gpsimd
    def _(pool):
        pool.wait_ge(s["slots_ready"], 1)
        for k in range(2):
            for t in range(B):
                pool.indirect_dma_start(out=xg, out_offset=bass.IndirectOffsetOnAxis(ap=slots[0:S, k, t:t + 1], axis=0),
                                        in_=xh_moe[:, t, :], in_offset=None).then_inc(s["scattered"], 16)
        pool.wait_ge(s["scattered"], 16 * 2 * B)

    @block.vector
    def _(v):
        done, n = s["dve"], Count()
        V = nc.vector

        def wide(ap):
            return ap.unsqueeze(2).to_broadcast([S, B, E])

        def over_tokens(ap):
            return ap.unsqueeze(1).to_broadcast([S, B, E])

        V.memset(both[:, 0:B, :], 0.0)
        v.wait_ge(s["consts_in"], 16 * 5)
        V.tensor_reduce(top[:], logits[:], axis=AX_X, op=ALU.max).then_inc(done, 1)
        v.wait_ge(done, n())
        V.tensor_tensor(gates[:], logits[:], wide(top[:]), ALU.subtract).then_inc(s["sub_ready"], 1)
        v.wait_ge(s["exp_ready"], 1)
        V.tensor_reduce(top[:], gates[:], axis=AX_X, op=ALU.add).then_inc(done, 1)
        v.wait_ge(done, n())
        V.reciprocal(top[:], top[:]).then_inc(done, 1)
        v.wait_ge(done, n())
        V.tensor_tensor(gates[:], gates[:], wide(top[:]), ALU.mult).then_inc(done, 1)
        v.wait_ge(done, n())
        for weight, one in ((weight1, one1), (weight2, one2)):
            V.tensor_reduce(weight[:], gates[:], axis=AX_X, op=ALU.max).then_inc(done, 1)
            v.wait_ge(done, n())
            V.tensor_tensor(hit[:], gates[:], wide(weight[:]), ALU.is_ge).then_inc(done, 1)
            v.wait_ge(done, n())
            V.tensor_scalar(hit[:], hit[:], -float(E), float(E), ALU.mult, ALU.add).then_inc(done, 1)
            v.wait_ge(done, n())
            V.tensor_tensor(cand[:], hit[:], over_tokens(iota[:]), ALU.add).then_inc(done, 1)
            v.wait_ge(done, n())
            V.tensor_reduce(index[:], cand[:], axis=AX_X, op=ALU.min).then_inc(done, 1)
            v.wait_ge(done, n())
            V.tensor_tensor(one[:], over_tokens(iota[:]), wide(index[:]), ALU.is_equal).then_inc(done, 1)
            v.wait_ge(done, n())
            if one is one1:
                V.scalar_tensor_tensor(gates[:].rearrange("p b e -> p (b e)"), one1[:].rearrange("p b e -> p (b e)"), -2.0,
                                       gates[:].rearrange("p b e -> p (b e)"), ALU.mult, ALU.add).then_inc(done, 1)
                v.wait_ge(done, n())
        V.tensor_tensor(both[:, B:2 * B, :], one1[:], one2[:], ALU.add).then_inc(s["both_ready"], 1)
        v.wait_ge(s["pos_ps"], 1)
        V.tensor_copy(count[:], bank[7][0:S, TE:TE + E]).then_inc(done, 1)
        v.wait_ge(done, n())
        V.tensor_tensor(over[:], count[:].unsqueeze(2).to_broadcast([S, E, NT_E]),
                        steps[:].unsqueeze(1).to_broadcast([S, E, NT_E]), ALU.is_gt).then_inc(done, 1)
        v.wait_ge(done, n())
        V.tensor_reduce(ntile[:], over[:], axis=AX_X, op=ALU.add).then_inc(done, 1)
        v.wait_ge(done, n())
        V.tensor_tensor(prod[:], lower[:], ntile[:].unsqueeze(1).to_broadcast([S, E, E]), ALU.mult).then_inc(done, 1)
        v.wait_ge(done, n())
        V.tensor_reduce(first[:], prod[:], axis=AX_X, op=ALU.add).then_inc(done, 1)
        v.wait_ge(done, n())
        V.tensor_scalar(first128[:], first[:], float(P), None, ALU.mult).then_inc(done, 1)
        v.wait_ge(done, n())
        V.tensor_tensor(slot[:], bank[7][0:S, 0:TE].rearrange("p (b e) -> p b e", e=E), over_tokens(first128[:]), ALU.add).then_inc(done, 1)
        v.wait_ge(done, n())
        for k, one in enumerate((one1, one2)):
            V.tensor_tensor(cand[:], one[:], slot[:], ALU.mult).then_inc(done, 1)
            v.wait_ge(done, n())
            V.tensor_reduce(slot_f[:, k, :], cand[:], axis=AX_X, op=ALU.add).then_inc(done, 1)
            v.wait_ge(done, n())
        V.tensor_copy(slots[:], slot_f[:]).then_inc(s["slots_ready"], 1)
        V.tensor_tensor(started[:], tiles[:].unsqueeze(1).to_broadcast([S, E - 1, NTILE]),
                        first[:, 1:E].unsqueeze(2).to_broadcast([S, E - 1, NTILE]), ALU.is_ge).then_inc(done, 1)
        v.wait_ge(done, n())
        V.tensor_reduce(expert_f[:], started[:].rearrange("p e t -> p t e"), axis=AX_X, op=ALU.add).then_inc(done, 1)
        v.wait_ge(done, n())
        V.tensor_copy(expert_row[:], expert_f[0:1, :]).then_inc(done, 1)
        n()
        def turn(i):
            for q in range(2):
                at = i * 2 + (q + 1)
                v.wait_ge(s["k1_ready"], at)
                V.tensor_tensor(kr[:, q, :, :], ps[:, 2 * q:2 * q + 2, 0:KP], ka[:, q, 0, :, :], ALU.subtract).then_inc(s["k_read"], 1)
                v.wait_ge(s["k_read"], at)
                V.tensor_copy(ka[:, q, 1, :, :], kr[:, q, :, :]).then_inc(s["k2_ready"], 1)
                v.wait_ge(s["k2_ready"], at)
                V.tensor_tensor(ka[:, q, 2, :, :], kr[:, q, :, :], ka[:, q, 1, :, :], ALU.subtract).then_inc(s["k3_ready"], 1)

        with v.Fori(0, B // 2) as i:
            turn(i)

    @block.scalar
    def _(a):
        a.wait_ge(s["sub_ready"], 1)
        nc.scalar.activation(gates[:], gates[:], ACT.Exp).then_inc(s["exp_ready"], 1)
        def turn(i, first):
            for dst, name in zip(weights[1:], ("rw2", "rw3")):
                a.dma_start(dst[:, i, :, :], dram[name][i].rearrange("(c p) n -> p c n", p=P)).then_inc(s["experts_in"], 16)
            for q in range(2):
                at = i * 2 + (q + 1)
                a.wait_ge(s["k_ps"], at)
                if not first:
                    a.wait_ge(s[f"k_out{q}"], i * 32)
                nc.scalar.activation(ka[:, q, 0, :, :], ps[:, 2 * q:2 * q + 2, 0:KP], ACT.Copy).then_inc(s["k1_ready"], 1)

        for dst, name in zip(biases, ("rb1", "rb2", "rb3")):
            a.dma_start(dst[:], dram[name].rearrange("(o e) n -> o e n", o=1).to_broadcast([P, E, dst.shape[2]])).then_inc(s["experts_in"], 16)
        turn(0, True)
        with a.Fori(1, B // 2) as i:
            turn(i, False)
        a.wait_ge(s["experts_in"], 16 * (2 * E + 3))

    @block.tensor
    def _(t):
        mm = nc.tensor.matmul

        def keys(b, q, arrived, first):
            t.wait_ge(s[f"ctx_in{q}"], arrived)
            if not first:
                t.wait_ge(s["k_read"], b - 1)
            for m in range(C):
                for c in range(C):
                    last = mm(ps[:, 2 * (q % 2) + m, 0:KP], wk1[:, c, m * P:(m + 1) * P], cT[:, q, c, :], start=c == 0, stop=c == C - 1)
            last.then_inc(s["k_ps"], 1)

        t.wait_ge(s["weights_in"], 16)
        for q in range(2):
            keys(q, q, 16, True)
        t.wait_ge(s["consts_in"], 16 * 5)
        t.wait_ge(s["both_ready"], 1)
        row = both[:].rearrange("p b e -> p (b e)")
        mm(bank[7][0:S, 0:TE], before[:], row[:, TE:2 * TE], start=True, stop=False)
        for k in range(1, B):
            last = mm(bank[7][0:S, 0:TE], ones[0:S, 0:S], row[:, TE - k * E:2 * TE - k * E], start=False, stop=k == B - 1)
        for k in range(B):
            last = mm(bank[7][0:S, TE:TE + E], ones[0:S, 0:S], row[:, TE + k * E:TE + (k + 1) * E], start=k == 0, stop=k == B - 1)
        last.then_inc(s["pos_ps"], 1)

        for q in range(2, 4):
            keys(q, q, 16, False)
        with t.Fori(1, B // 4) as i:
            for q in range(4):
                keys(i * 4 + q, q, (i + 1) * 16, False)


def routed_experts(nc, ctx, dram, expert_row, weights, biases, ps, bank, ident, always, new_semaphore):

    def sb(name, shape, dt=F32):
        return ctx.enter_context(nc.sbuf_tensor(name, shape, dt))

    def sem(name):
        return new_semaphore(name)

    rw1, rw2, rw3 = weights
    rb1, rb2, rb3 = biases
    rows = sb("rows", [P, 2, D])
    rowsT = sb("rowsT", [P, 2, C * P])
    h1 = sb("h1", [P, 2, H])
    h2 = sb("h2", [P, 2, H])
    act1 = sb("act1", [P, 2, H])
    glu = sb("glu", [P, 2, H])
    gT = sb("gT", [P, 2, H])
    y = sb("y", [P, 2, D])
    s = {n: sem("c_" + n) for n in (
        "rows_in0", "rows_in1", "rT_ps", "rT_ready", "p1_ps", "p2_ps", "h1_ready", "silu_ready", "h2_ready",
        "glu_ready", "gT_ps", "gT_ready", "y_ps", "y_ready", "y_out0", "y_out1")}
    xg, yscr = dram["xg"], dram["yscr"]
    LAST = NTILE - 1
    block = ctx.enter_context(nc.Block())

    @block.sync
    def _(sp):
        def load(n, q, first=False):
            if not first:
                sp.wait_ge(s["rT_ps"], n - 1)
            sp.dma_start(rows[:, q, :], xg[bass.ds(n * P, P), :]).then_inc(s[f"rows_in{q}"], 16)

        load(0, 0, True)
        load(1, 1, True)
        with sp.Fori(1, NTILE // 2) as i:
            for q in range(2):
                load(i * 2 + q, q)

    @block.gpsimd
    def _(pool):
        with pool.Fori(0, NTILE // 2) as i:
            for q in range(2):
                n = i * 2 + q
                wait_alone(pool, always, s["y_ready"], n + 1)
                pool.dma_start(yscr[bass.ds(n * P, P), :], y[:, q, :]).then_inc(s[f"y_out{q}"], 16)
        for q in range(2):
            pool.wait_ge(s[f"y_out{q}"], 16 * (NTILE // 2))

    @block.vector
    def _(v):
        V = nc.vector

        def expert(n):
            return v.value_load(expert_row[0:1, bass.ds(n, 1)], min_val=0, max_val=E - 1)

        def front(n, q):
            e = expert(n)
            v.wait_ge(s["p1_ps"], n + 1)
            V.tensor_tensor(h1[:, q, :], bank[1 + 2 * q], rb1[:, e, :], ALU.add).then_inc(s["h1_ready"], 1)
            v.wait_ge(s["p2_ps"], n + 1)
            V.tensor_tensor(h2[:, q, :], bank[2 + 2 * q], rb2[:, e, :], ALU.add).then_inc(s["h2_ready"], 1)
            v.wait_ge(s["silu_ready"], n + 1)
            v.wait_ge(s["h2_ready"], n + 1)
            V.tensor_tensor(glu[:, q, :], act1[:, q, :], h2[:, q, :], ALU.mult).then_inc(s["glu_ready"], 1)

        def back(n, q, turn):
            e = expert(n)
            if turn is not None:
                v.wait_ge(s[f"y_out{q}"], turn * 16)
            v.wait_ge(s["y_ps"], n + 1)
            V.tensor_tensor(y[:, q, :], bank[6][:, 0:D], rb3[:, e, :], ALU.add).then_inc(s["y_ready"], 1)

        front(0, 0)
        front(1, 1)
        back(0, 0, None)
        front(2, 0)
        back(1, 1, None)
        with v.Fori(1, NTILE // 2 - 1) as i:
            front(i * 2 + 1, 1)
            back(i * 2, 0, i)
            front(i * 2 + 2, 0)
            back(i * 2 + 1, 1, i)
        front(LAST, 1)
        back(LAST - 1, 0, NTILE // 2 - 1)
        back(LAST, 1, NTILE // 2 - 1)

    @block.scalar
    def _(a):
        A = nc.scalar.activation

        def rowsT_out(n, q):
            a.wait_ge(s["rT_ps"], n + 1)
            A(rowsT[:, q, :], bank[0][:, 0:C * P], ACT.Copy).then_inc(s["rT_ready"], 1)

        def gT_out(n, q):
            a.wait_ge(s["gT_ps"], n + 1)
            A(gT[:, q, :], bank[5], ACT.Copy).then_inc(s["gT_ready"], 1)

        def silu(n, q):
            a.wait_ge(s["h1_ready"], n + 1)
            A(act1[:, q, :], h1[:, q, :], ACT.Silu).then_inc(s["silu_ready"], 1)

        rowsT_out(0, 0)
        rowsT_out(1, 1)
        silu(0, 0)
        with a.Fori(0, NTILE // 2 - 1) as i:
            for k in range(2):
                rowsT_out(i * 2 + 2 + k, k)
                gT_out(i * 2 + k, k)
                silu(i * 2 + 1 + k, 1 - k)
        gT_out(LAST - 1, 0)
        silu(LAST, 1)
        gT_out(LAST, 1)

    @block.tensor
    def _(t):
        mm = nc.tensor.matmul

        def rows_T(n, q, turn):
            t.wait_ge(s[f"rows_in{q}"], (turn + 1) * 16)
            if not (isinstance(n, int) and n == 0):
                t.wait_ge(s["rT_ready"], n)
            for c in range(C):
                last = nc.tensor.transpose(bank[0][:, c * P:(c + 1) * P], rows[:, q, c * P:(c + 1) * P], ident[:])
            last.then_inc(s["rT_ps"], 1)

        def up(n, q):
            e = t.value_load(expert_row[0:1, bass.ds(n, 1)], min_val=0, max_val=E - 1)
            t.wait_ge(s["rT_ready"], n + 1)
            for k, (w, sign) in enumerate(((rw1, "p1_ps"), (rw2, "p2_ps"))):
                for c in range(C):
                    last = mm(bank[1 + 2 * q + k], rowsT[:, q, c * P:(c + 1) * P], w[:, e, c, :], start=c == 0, stop=c == C - 1)
                last.then_inc(s[sign], 1)

        def hidden_T(n, q):
            t.wait_ge(s["glu_ready"], n + 1)
            for m in range(HM):
                last = nc.tensor.transpose(bank[5][:, m * P:(m + 1) * P], glu[:, q, m * P:(m + 1) * P], ident[:])
            last.then_inc(s["gT_ps"], 1)

        def down(n, q):
            e = t.value_load(expert_row[0:1, bass.ds(n, 1)], min_val=0, max_val=E - 1)
            t.wait_ge(s["gT_ready"], n + 1)
            if not (isinstance(n, int) and n == 0):
                t.wait_ge(s["y_ready"], n)
            for m in range(HM):
                last = mm(bank[6][:, 0:D], gT[:, q, m * P:(m + 1) * P], rw3[:, e, m, :], start=m == 0, stop=m == HM - 1)
            last.then_inc(s["y_ps"], 1)

        def step(n, q, turn):
            rows_T(n + 1, 1 - q, turn)
            hidden_T(n - 1, 1 - q)
            up(n, q)
            down(n - 1, 1 - q)

        rows_T(0, 0, 0)
        rows_T(1, 1, 0)
        up(0, 0)
        step(1, 1, 1)
        step(2, 0, 1)
        with t.Fori(1, NTILE // 2 - 1) as i:
            step(i * 2 + 1, 1, i + 1)
            step(i * 2 + 2, 0, i + 1)
        hidden_T(LAST - 1, 0)
        up(LAST, 1)
        down(LAST - 1, 0)
        hidden_T(LAST, 1)
        down(LAST, 1)


def layer1(nc, ctx, dram, out, x_res, weight1, weight2, slots, ps, bank, ident, ones, always, new_semaphore):

    def sb(name, shape, dt=F32):
        return ctx.enter_context(nc.sbuf_tensor(name, shape, dt))

    def sem(name):
        return new_semaphore(name)

    DEPTH = 3 * 2 * HD
    QUAD = 4
    yscr, kscr, vscr, qscr, mscr = (dram[n] for n in ("yscr", "kscr", "vscr", "qscr", "mscr"))
    wq1 = sb("wq1", [P, C, D])
    wo1 = sb("wo1", [P, C, D])
    wf = sb("wf", [P, C, D])
    vrT = sb("vrT", [32, D])
    cfT = sb("cfT", [32, D])
    bf_row = sb("bf_row", [1, D])
    half = sb("d_half", [S, G])
    yg = sb("yg", [S, B, 2, D])
    stat = sb("d_stat", [S, G, 6])
    mv = sb("d_mv", [S, G, 2])
    rstd = sb("d_rstd", [S, G])
    xh = sb("d_xh", [S, G, D])
    xhT = sb("d_xhT", [P, C, GS])
    qa = sb("qa", [P, 3, C, GS], BF16)
    qr = sb("qr", [P, C, GS])
    kst = sb("kst", [P, 4, NH, KP], BF16)
    qst = sb("qst", [P, 4, NH, S], BF16)
    vt = sb("vt", [KC, 2, NKC, NH, HD + 1])
    mxh = sb("mxh", [S, NH])
    mr = sb("mr", [S, 2, NH])
    mparts = sb("mparts", [S, 2, 3, NH], BF16)
    identb = sb("identb", [P, P], BF16)
    mT = sb("mT", [3 * NH, 2, S], BF16)
    outT = sb("outT", [P, QUAD, S])
    pT = sb("d_pT", [KC, 2, NKC, QUAD * S])
    rec = sb("rec", [S, NH])
    heads = sb("heads", [S, B, D])
    res = sb("res", [S, G, D])
    hk = sb("hk", [S, G, D])
    hT = sb("hT", [P, C, GS])

    s = {n: sem("d_" + n) for n in (
        "weights_in", "consts_ready", "y_in0", "y_in1", "y_in2", "y_in3", "qs_in0", "qs_in1", "qs_in2", "qs_in3", "wf_ps", "wf_ready", "dve", "pool", "mixed", "mv_ready",
        "rstd_ready", "xh_ready", "q_read", "q2_ready", "q3_ready", "q_out",
        "k_in0", "k_in1", "k_in2", "k_in3", "v_in0", "v_in1",
        "s_ps", "s_max", "m_ready", "mT_ps", "mT_ready", "m_out0", "m_out1", "mrow_in0", "mrow_in1", "mrow_in2", "mrow_in3",
        "st_ps", "p_ready", "pv_ps", "outT_ready", "out_ps", "heads_ready", "h_kept", "hT_ps", "hT_ready", "o_ps", "x3_ready",
        "mv3_ready", "rstd3_ready", "xh3_ready", "x3T_ps", "x3T_ready", "f_ps", "res_ready", "res_out0", "res_out1", "res_out2", "res_out3",
        "half_ready", "xhT_ps", "xhT_ready", "q_ps", "q1_ready")}
    block = ctx.enter_context(nc.Block())

    def rstd_of(pool, ready, n, done, steps):
        wait_alone(pool, always, ready, n)
        pool.tensor_scalar(rstd[:], mv[:, :, 1], EPS, None, ALU.add).then_inc(s["pool"], 1)
        pool.wait_ge(s["pool"], steps)
        pool.tensor_tensor(rstd[:], rstd[:], half[:], ALU.pow).then_inc(done, 1)

    def o_of(j):
        return bank[2 + j // 2][0:S, (j % 2) * D:(j % 2 + 1) * D]

    def f_of(j):
        return bank[6 + j // 2][0:S, (j % 2) * D:(j % 2 + 1) * D]

    PAIRS = ((0, 0), (1, 0), (2, 0), (0, 1), (1, 1), (0, 2))

    @block.sync
    def _(sp):
        for dst, name in ((wq1, "wq1_t"), (wo1, "wo1_t"), (wf, "wf_t")):
            sp.dma_start(dst[:], dram[name].rearrange("(c p) n -> p c n", p=P)).then_inc(s["weights_in"], 16)
        for dst, name in ((vrT, "vr_t"), (cfT, "cf_t")):
            sp.dma_start(dst[:], dram[name]).then_inc(s["weights_in"], 16)
        sp.dma_start(bf_row[:], dram["bf"].rearrange("(o n) -> o n", o=1)).then_inc(s["weights_in"], 16)

        def load_keys(b, slot):
            for r, (k, _) in enumerate(PAIRS):
                sp.dma_start(kst[r * HD:(r + 1) * HD, slot, :, :], kscr[b, k].rearrange("(h p) t -> p h t", p=HD)).then_inc(s[f"k_in{slot}"], 16)

        def load_queries(i, j):
            for r, (_, k) in enumerate(PAIRS):
                sp.dma_start(qst[r * HD:(r + 1) * HD, j, :, :],
                             qscr[i, k][:, j * S:(j + 1) * S].rearrange("(h p) t -> p h t", p=HD)).then_inc(s[f"qs_in{j}"], 16)

        def load_values(b, slot):
            sp.dma_start(vt[:, slot, :, :, :].rearrange("p c h d -> p (c h d)"), vscr[b]).then_inc(s[f"v_in{slot}"], 16)

        for b in range(4):
            load_keys(b, b)
        for b in range(2):
            load_values(b, b)
        with sp.Fori(0, NG) as i:
            sp.wait_ge(s["q3_ready"], i + 1)
            for m in range(C):
                sp.dma_start(qscr[i][:, m * P:(m + 1) * P, :].rearrange("s f t -> f s t"), qa[:, :, m, :]).then_inc(s["q_out"], 16)
            wait_alone(sp, always, s["q_out"], (i + 1) * 32)
        for j in range(4):
            load_queries(0, j)

        def ahead_in_turn(i, j):
            sp.wait_ge(s["mT_ready"], i * 4 + (j + 1))
            sp.dma_start(mscr[i * 4 + j], mT[:, j % 2, :]).then_inc(s[f"m_out{j % 2}"], 16)
            sp.wait_ge(s[f"m_out{j % 2}"], (i * 2 + (j // 2 + 1)) * 16)
            sp.dma_start(qst[DEPTH:DEPTH + 3, j, :, :], mscr[i * 4 + j].rearrange("(s h) q -> s h q", h=NH)).then_inc(s[f"mrow_in{j}"], 16)

        sp.wait_ge(s["consts_ready"], 2)
        ahead_in_turn(0, 0)
        ahead_in_turn(0, 1)

        def turn(i, last):
            for j in range(4):
                if j < 2:
                    ahead_in_turn(i, j + 2)
                elif not last:
                    ahead_in_turn(i + 1, j - 2)
                if not last or j < 2:
                    sp.wait_ge(s["pv_ps"], i * 4 + (j + 1))
                    load_values(i * 4 + (j + 2), j % 2)
                if not last:
                    load_keys(i * 4 + (j + 4), j)
                    load_queries(i + 1, j)

        with sp.Fori(0, NG - 1) as i:
            turn(i, False)
        turn(NG - 1, True)
        with sp.Fori(0, NG) as i:
            for j in range(G):
                sp.wait_ge(s["res_ready"], i * G + (j + 1))
                sp.dma_start(out[i * G + j], res[:, j, :]).then_inc(s[f"res_out{j}"], 16)
        for j in range(G):
            sp.wait_ge(s[f"res_out{j}"], 16 * NG)

    @block.gpsimd
    def _(pool):
        pool.memset(half[:], -0.5).then_inc(s["half_ready"], 1)
        pool.wait_ge(s["half_ready"], 1)
        for i in range(NG):
            for j in range(G):
                b = i * G + j
                if i:
                    pool.wait_ge(s[f"y_in{j}"], i * 32)
                for k in range(2):
                    pool.indirect_dma_start(out=yg[:, b, k, :], out_offset=None, in_=yscr,
                                            in_offset=bass.IndirectOffsetOnAxis(ap=slots[0:S, k, b:b + 1], axis=0)).then_inc(s[f"y_in{j}"], 16)
            if i:
                rstd_of(pool, s["mv_ready"], i, s["rstd_ready"], i)
        rstd_of(pool, s["mv_ready"], NG, s["rstd_ready"], NG)
        with pool.Fori(0, NG) as i:
            rstd_of(pool, s["mv3_ready"], i + 1, s["rstd3_ready"], i + (NG + 1))

    @block.vector
    def _(v):
        V, done = nc.vector, s["dve"]
        for stack in (kst, qst):
            V.memset(stack[DEPTH:P, :, :, :].rearrange("p j h t -> p (j h t)").bitcast(F32), 0.0).then_inc(s["consts_ready"], 1)
        v.wait_ge(s["weights_in"], 16 * 6)
        v.wait_ge(s["wf_ps"], 1)
        V.tensor_tensor(wf[:], wf[:], ps[:, 0:C, 0:D], ALU.add).then_inc(s["wf_ready"], 1)
        V.tensor_copy(identb[:], ident[:]).then_inc(s["wf_ready"], 1)

        def mean_var(src, ready, n):
            for j in range(G):
                V.bn_stats(stat[:, j, :], src(j)).then_inc(done, 1)
                n()
            for j in range(G):
                wait_alone(v, always, done, n.now() - (G - 1 - j))
                if j < G - 1:
                    V.bn_aggr(mv[:, j, :], stat[:, j, :])
                else:
                    V.bn_aggr(mv[:, j, :], stat[:, j, :]).then_inc(ready, 1)

        PER = 2 * G

        def combine(i):
            n = Count(i, PER)
            for k, w in enumerate((weight1, weight2)):
                for j in range(G):
                    b = i * G + j
                    if k == 0:
                        v.wait_ge(s[f"y_in{j}"], (i + 1) * 32)
                    else:
                        v.wait_ge(done, n.now() - (G - 1 - j))
                    V.scalar_tensor_tensor(x_res[:, b, :], yg[:, b, k, :], w[:, bass.ds(b, 1)], x_res[:, b, :],
                                           ALU.mult, ALU.add).then_inc(done if k == 0 else s["mixed"], 1)
                    if k == 0:
                        n()
            wait_alone(v, always, s["mixed"], i * G + G)
            mean_var(lambda j: x_res[:, i * G + j, :], s["mv_ready"], n)
            assert n.n == PER

        def normalized(i):
            v.wait_ge(s["mv_ready"], i + 1)
            v.wait_ge(s["rstd_ready"], i + 1)
            for j in range(G):
                V.tensor_scalar(xh[:, j, :], x_res[:, i * G + j, :], mv[:, j, 0:1], rstd[:, j:j + 1],
                                ALU.subtract, ALU.mult).then_inc(s["xh_ready"], 1)

        def split_queries(i):
            v.wait_ge(s["q1_ready"], i * C + C)
            for m in range(C):
                V.scalar_tensor_tensor(qr[:, m, :], bank[2 + m][:, 0:GS], 0.25, qa[:, 0, m, :], ALU.mult, ALU.subtract).then_inc(s["q_read"], 1)
            v.wait_ge(s["q_read"], i * C + C)
            V.tensor_copy(qa[:, 1, :, :], qr[:]).then_inc(s["q2_ready"], 1)
            v.wait_ge(s["q2_ready"], i + 1)
            V.tensor_tensor(qa[:, 2, :, :], qr[:], qa[:, 1, :, :], ALU.subtract).then_inc(s["q3_ready"], 1)

        combine(0)
        normalized(0)
        with v.Fori(1, NG) as i:
            combine(i)
            split_queries(i - 1)
            normalized(i)
        split_queries(NG - 1)

        def maximum(b, g, at):
            v.wait_ge(s["s_ps"], b * 8 + (g + 1))
            V.tensor_reduce(mxh[:, 2 * g:2 * g + 2], ps[0:S, 2 * (g % 2):2 * (g % 2) + 2, 0:K], axis=AX_X, op=ALU.max).then_inc(s["s_max"], 1)

        def negated_parts(b, slot):
            base = b * 4
            v.wait_ge(s["s_max"], b * 8 + 8)
            V.tensor_scalar(mparts[:, slot, 0, :], mxh[:], -1.0, None, ALU.mult).then_inc(s["m_ready"], 1)
            v.wait_ge(s["m_ready"], base + 1)
            V.scalar_tensor_tensor(mr[:, slot, :], mxh[:], -1.0, mparts[:, slot, 0, :], ALU.mult, ALU.subtract).then_inc(s["m_ready"], 1)
            v.wait_ge(s["m_ready"], base + 2)
            V.tensor_copy(mparts[:, slot, 1, :], mr[:, slot, :]).then_inc(s["m_ready"], 1)
            v.wait_ge(s["m_ready"], base + 3)
            V.tensor_tensor(mparts[:, slot, 2, :], mr[:, slot, :], mparts[:, slot, 1, :], ALU.subtract).then_inc(s["m_ready"], 1)
            v.wait_ge(s["mT_ps"], b + 1)

        def turned(b, slot):
            V.tensor_copy(mT[:, slot, :], ps[0:3 * NH, 0, 0:S // 2].bitcast(BF16)).then_inc(s["mT_ready"], 1)

        def first_pass(b, slot, before=None, free=None):
            for g in range(8):
                maximum(b, g, slot)
                if g == 2 and before is not None:
                    finish(before)
            negated_parts(b, slot)
            if free is not None:
                v.wait_ge(s[f"m_out{slot}"], free)
            turned(b, slot)

        def finish(b):
            v.wait_ge(s["out_ps"], b + 1)
            out_ps = bank[7][0:S, :].rearrange("p (h d) -> p h d", d=32)
            V.reciprocal(rec[:].unsqueeze(2), out_ps[:, :, HD:HD + 1]).then_inc(s["heads_ready"], 1)
            v.wait_ge(s["heads_ready"], b * 2 + 1)
            V.tensor_tensor(heads[:, b, :].rearrange("p (h d) -> p h d", d=HD), out_ps[:, :, 0:HD],
                            rec[:].unsqueeze(2).to_broadcast([S, NH, HD]), ALU.mult).then_inc(s["heads_ready"], 1)

        V.memset(bank[7][:], 0.0).then_inc(s["wf_ready"], 1)
        first_pass(0, 0)
        first_pass(1, 1)

        def turn(i, first, last):
            for j in range(4):
                b = i * 4 + j
                before = None if first and j == 0 else b - 1
                if not last or j < 2:
                    first_pass(b + 2, j % 2, before, (i * 2 + (j // 2 + 1)) * 16)
                else:
                    finish(before)

        turn(0, True, False)
        with v.Fori(1, NG - 1) as i:
            turn(i, False, False)
        turn(NG - 1, False, True)
        finish(B - 1)

        def attended(i):
            n = Count(i, G, NG * PER)
            for j in range(G):
                v.wait_ge(s["o_ps"], i * G + (2 * (j // 2) + 2))
                V.tensor_tensor(x_res[:, i * G + j, :], o_of(j), x_res[:, i * G + j, :], ALU.add).then_inc(s["x3_ready"], 1)
            wait_alone(v, always, s["x3_ready"], i * G + G)
            mean_var(lambda j: x_res[:, i * G + j, :], s["mv3_ready"], n)

        def normalized3(i):
            v.wait_ge(s["mv3_ready"], i + 1)
            v.wait_ge(s["rstd3_ready"], i + 1)
            for j in range(G):
                V.tensor_scalar(xh[:, j, :], x_res[:, i * G + j, :], mv[:, j, 0:1], rstd[:, j:j + 1],
                                ALU.subtract, ALU.mult).then_inc(s["xh3_ready"], 1)

        def results(i, first):
            for j in range(G):
                v.wait_ge(s["f_ps"], i * G + (2 * (j // 2) + 2))
                if not first:
                    v.wait_ge(s[f"res_out{j}"], i * 16)
                V.tensor_tensor(res[:, j, :], f_of(j), x_res[:, i * G + j, :], ALU.add).then_inc(s["res_ready"], 1)

        def turn(i, first):
            normalized3(i - 1)
            attended(i)
            results(i - 1, first)

        attended(0)
        turn(1, True)
        with v.Fori(2, NG) as i:
            turn(i, False)
        normalized3(NG - 1)
        results(NG - 1, False)

    @block.scalar
    def _(a):
        A = nc.scalar.activation
        def queries(i, first):
            for c in range(C):
                a.wait_ge(s["xhT_ps"], i * C + (c + 1))
                A(xhT[:, c, :], bank[c][:, 0:GS], ACT.Copy).then_inc(s["xhT_ready"], 1)
            for m in range(C):
                a.wait_ge(s["q_ps"], i * C + (m + 1))
                if m == 0 and not first:
                    a.wait_ge(s["q_out"], i * 32)
                A(qa[:, 0, m, :], bank[2 + m][:, 0:GS], ACT.Copy, scale=0.25).then_inc(s["q1_ready"], 1)

        def ones_under_keys(slot):
            A(kst[DEPTH:DEPTH + 3, slot, :, :], kst[DEPTH:DEPTH + 3, slot, :, :], ACT.Copy, bias=1.0, scale=0.0).then_inc(s["consts_ready"], 1)

        queries(0, True)
        a.wait_ge(s["consts_ready"], 2)
        ones_under_keys(0)
        with a.Fori(1, NG) as i:
            queries(i, False)
        for slot in range(1, 4):
            ones_under_keys(slot)

        def exps(b, q):
            for k in range(NKC):
                a.wait_ge(s["st_ps"], (b * 4 + q) * NKC + (k + 1))
                A(pT[:, q % 2, k, :], bank[4 + k][0:KC, 0:QUAD * S], ACT.Exp).then_inc(s["p_ready"], 1)

        def keep_outputs(b):
            a.wait_ge(s["pv_ps"], b + 1)
            A(outT[:].rearrange("p q t -> p (q t)"), bank[7][:, 0:GS], ACT.Copy).then_inc(s["outT_ready"], 1)

        for q in range(4):
            exps(0, q)
        with a.Fori(1, B) as b:
            for q in range(4):
                exps(b, q)
                if q == 0:
                    keep_outputs(b - 1)
        keep_outputs(B - 1)

        def keep_heads(i):
            wait_alone(a, always, s["heads_ready"], i * (2 * G) + 2 * G)
            A(hk[:], heads[:, bass.ds(i * G, G), :], ACT.Copy).then_inc(s["h_kept"], 1)

        def keep_turned(i, banks, dst, turned, kept):
            for c in range(C):
                a.wait_ge(s[turned], i * C + (c + 1))
                A(dst[:, c, :], banks[c][:, 0:GS], ACT.Copy).then_inc(s[kept], 1)

        keep_heads(0)
        keep_turned(0, bank[0:2], hT, "hT_ps", "hT_ready")
        with a.Fori(1, NG) as i:
            keep_heads(i)
            keep_turned(i, bank[0:2], hT, "hT_ps", "hT_ready")
            keep_turned(i - 1, bank[4:6], xhT, "x3T_ps", "x3T_ready")
        keep_turned(NG - 1, bank[4:6], xhT, "x3T_ps", "x3T_ready")

    @block.tensor
    def _(t):
        mm = nc.tensor.matmul

        def turn_over(src, sign, banks):
            for c in range(C):
                for j in range(G):
                    last = nc.tensor.transpose(banks[c][:, j * S:(j + 1) * S], src[:, j, c * P:(c + 1) * P], ident[0:S, 0:S])
                last.then_inc(sign, 1)

        t.wait_ge(s["weights_in"], 16 * 6)
        for c in range(C):
            last = mm(bank[c][:, 0:D], vrT[:, c * P:(c + 1) * P], cfT[:], start=True, stop=True)
        last.then_inc(s["wf_ps"], 1)
        t.wait_ge(s["wf_ready"], 2)
        with t.Fori(0, NG) as i:
            t.wait_ge(s["xh_ready"], i * G + G)
            turn_over(xh, s["xhT_ps"], bank[0:2])
            t.wait_ge(s["xhT_ready"], i * C + C)
            for m in range(C):
                for c in range(C):
                    last = mm(bank[2 + m][:, 0:GS], wq1[:, c, m * P:(m + 1) * P], xhT[:, c, :], start=c == 0, stop=c == C - 1)
                last.then_inc(s["q_ps"], 1)

        def scores(b, slot, g, free=True):
            if free:
                t.wait_ge(s["s_max"], b * 8 + (g - 1))
            for k in range(2):
                h = 2 * g + k
                last = mm(bank[2 * (g % 2) + k][0:S, 0:K], qst[0:DEPTH, slot, h, :], kst[0:DEPTH, slot, h, 0:K], start=True, stop=True)
            last.then_inc(s["s_ps"], 1)

        def maxima_T(b, slot):
            wait_alone(t, always, s["m_ready"], b * 4 + 4)
            nc.tensor.transpose(ps[0:3 * NH, 0, 0:S // 2].bitcast(BF16), mparts[:, slot % 2, :, :].rearrange("p s h -> p (s h)"),
                                identb[0:S, 0:S]).then_inc(s["mT_ps"], 1)

        def arrived(slot, count):
            t.wait_ge(s[f"k_in{slot}"], count * 6 * 16)
            t.wait_ge(s[f"qs_in{slot}"], count * 6 * 16)

        def transposed(b, slot, q, very_first):
            for k in range(NKC):
                if not very_first:
                    t.wait_ge(s["p_ready"], (b * 4 + (q - 1)) * NKC + (k + 1))
                for h in range(QUAD):
                    last = mm(bank[4 + k][:, h * S:(h + 1) * S], kst[:, slot, QUAD * q + h, k * KC:k * KC + P],
                              qst[:, slot, QUAD * q + h, :], start=True, stop=True)
                last.then_inc(s["st_ps"], 1)

        def outputs(b, slot, q):
            t.wait_ge(s["p_ready"], (b * 4 + q) * NKC + NKC)
            for k in range(NKC):
                for h in range(QUAD):
                    last = mm(bank[7][32 * h:32 * h + HD + 1, q * S:(q + 1) * S], vt[:, slot % 2, k, QUAD * q + h, :],
                              pT[:, q % 2, k, h * S:(h + 1) * S], start=k == 0, stop=k == NKC - 1)
            if q == 3:
                last.then_inc(s["pv_ps"], 1)

        def outputs_T(b):
            t.wait_ge(s["outT_ready"], b + 1)
            for q in range(QUAD):
                last = nc.tensor.transpose(bank[7][0:S, q * P:(q + 1) * P], outT[:, q, :], ident[:])
            last.then_inc(s["out_ps"], 1)

        t.wait_ge(s["wf_ready"], 3)
        t.wait_ge(s["q3_ready"], NG)
        for b in range(2):
            arrived(b, 1)
            for g in range(8):
                if b and g == 0:
                    t.wait_ge(s["mT_ready"], b)
                scores(b, b, g, b or g >= 2)
            maxima_T(b, b)

        def second(b, i, j, very_first, last):
            ahead = not last or j < 2
            if ahead:
                arrived((j + 2) % 4, i + (1 if j < 2 else 2))
                t.wait_ge(s["mT_ready"], b + 2)
            t.wait_ge(s[f"mrow_in{j}"], (i + 1) * 16)
            t.wait_ge(s[f"v_in{j % 2}"], (i * 2 + (j // 2 + 1)) * 16)
            for q in range(4):
                if ahead:
                    for g in range(2 * q, 2 * q + 2):
                        scores(b + 2, (j + 2) % 4, g)
                        if g == 2 and not very_first:
                            outputs_T(b - 1)
                elif q == 1:
                    outputs_T(b - 1)
                transposed(b, j, q, very_first and q == 0)
                if q == 0 and not very_first:
                    outputs(b - 1, (j - 1) % 4, 3)
                if q == 1 and not very_first:
                    t.wait_ge(s["heads_ready"], b * 2)
                if q:
                    outputs(b, j, q - 1)
            if ahead:
                maxima_T(b + 2, j)

        t.wait_ge(s["consts_ready"], 6)
        for j in range(4):
            second(j, 0, j, j == 0, False)
        with t.Fori(1, NG - 1) as i:
            for j in range(4):
                second(i * 4 + j, i, j, False, False)
        for j in range(4):
            second((NG - 1) * 4 + j, NG - 1, j, False, True)
        outputs(B - 1, 3, 3)
        outputs_T(B - 1)

        def attended(i, first=False):
            t.wait_ge(s["h_kept"], i + 1)
            turn_over(hk, s["hT_ps"], bank[0:2])
            t.wait_ge(s["hT_ready"], i * C + C)
            if not first:
                t.wait_ge(s["x3_ready"], i * G)
            for j in range(G):
                for c in range(C):
                    last = mm(o_of(j), hT[:, c, j * S:(j + 1) * S], wo1[:, c, :], start=c == 0, stop=c == C - 1)
                last.then_inc(s["o_ps"], 1)

        def mapped(i, first):
            t.wait_ge(s["xh3_ready"], i * G + G)
            turn_over(xh, s["x3T_ps"], bank[4:6])
            t.wait_ge(s["x3T_ready"], i * C + C)
            for j in range(G):
                if not first:
                    t.wait_ge(s["res_ready"], (i - 1) * G + (2 * (j // 2) + 2))
                for c in range(C):
                    mm(f_of(j), xhT[:, c, j * S:(j + 1) * S], wf[:, c, :], start=c == 0, stop=False)
                last = mm(f_of(j), ones[0:1, 0:S], bf_row[:], start=False, stop=True)
                last.then_inc(s["f_ps"], 1)

        attended(0, True)
        attended(1)
        mapped(0, True)
        with t.Fori(2, NG) as i:
            attended(i)
            mapped(i - 1, False)
        mapped(NG - 1, False)


def build_program(nc, dram, outs):
    ctx, semaphores = ExitStack(), ExitStack()
    with semaphores, ctx:
        def sb(name, shape, dt=F32):
            return ctx.enter_context(nc.sbuf_tensor(name, shape, dt))
        def sem(name):
            return ctx.enter_context(nc.semaphore(name))
        ps = ctx.enter_context(nc.psum_tensor("ps", [P, 8, 512], F32))
        bank = [ps[:, k, :] for k in range(8)]
        ident = sb("ident", [P, P])
        ones = sb("ones", [P, P])
        x_res = sb("x_res", [S, B, D])
        weight1 = sb("weight1", [S, B])
        weight2 = sb("weight2", [S, B])
        slots = sb("slots", [S, 2, B], I32)
        expert_row = sb("expert_row", [1, NTILE], I32)
        always = sem("always")
        used = []

        def sem_of(stack):
            def new_semaphore(name):
                used.append(stack.enter_context(nc.semaphore(name)))
                return used[-1]
            return new_semaphore

        def clear():
            with nc.Block() as block:
                @block.sync
                def _(sp):
                    for semaphore in used:
                        sp.sem_clear(semaphore)
            used.clear()

        nc.sync.sem_inc(always, 1)
        dram = dict(dram)
        for name, shape, dt in (
                ("xg", [NTILE * P, D], F32), ("yscr", [NTILE * P, D], F32), ("kscr", [B, 3, D, KP], BF16),
                ("vscr", [B, KC, NKC * NH * (HD + 1)], F32), ("qscr", [NG, 3, D, GS], BF16), ("mscr", [B, 3 * NH, S], BF16)):
            dram[name] = nc.dram_tensor(name, shape, dt, kind="Internal").ap()
        with ExitStack() as c_moe:
            xh_moe = c_moe.enter_context(nc.sbuf_tensor("xh_moe", [S, B, D], F32))
            logits = c_moe.enter_context(nc.sbuf_tensor("logits", [S, B, E], F32))
            rw1 = c_moe.enter_context(nc.sbuf_tensor("rw1", [P, E, C, H], F32))
            with ExitStack() as given_on:
                with ExitStack() as c0:
                    layer0(nc, c0, dram, x_res, xh_moe, logits, rw1, bank, ident, ones, always, sem_of(given_on))
                clear()
            weights = [rw1] + [c_moe.enter_context(nc.sbuf_tensor(f"rw{k}", shape, F32)) for k, shape in ((2, [P, E, C, H]), (3, [P, E, HM, D]))]
            biases = [c_moe.enter_context(nc.sbuf_tensor(f"rb{k}", [P, E, n], F32)) for k, n in ((1, H), (2, H), (3, D))]
            with ExitStack() as given_on:
                with ExitStack() as c1:
                    routing_and_projections(nc, c1, dram, xh_moe, logits, weight1, weight2, slots, expert_row,
                                            weights, biases, ps, bank, ones, always, sem_of(given_on))
                with ExitStack() as c2:
                    routed_experts(nc, c2, dram, expert_row, weights, biases, ps, bank, ident, always, sem_of(given_on))
                clear()
        with ExitStack() as c3:
            layer1(nc, c3, dram, outs["out"], x_res, weight1, weight2, slots, ps, bank, ident, ones, always, sem_of(semaphores))


def lay_out(inputs):
    import numpy as np
    a = {k: np.asarray(v) for k, v in inputs.items()}
    t = lambda w: np.ascontiguousarray(w.T)
    x0, f0, x1, f1 = "L0_xattn_", "L0_ffn_", "L1_xattn_", "L1_ffn_"
    ctx_t = np.zeros((B, D, KP), np.float32)
    ctx_t[:, :, :K] = a["ctx_1024"].transpose(0, 2, 1)
    out = {
        "x": a["x"], "ctx": a["ctx_1024"], "ctx_t": ctx_t, "mask": a["mask_Bx1xS2_ik1"],
        "wq_t": t(a[x0 + "Wq"]), "wk_t": t(a[x0 + "Wk"]), "wv_t": t(a[x0 + "Wv"]), "wo0": a[x0 + "Wo"],
        "identity": np.eye(P, dtype=np.float32), "ones": np.ones((P, P), np.float32),
    }
    out["wk1_t"], out["wv1_t"], out["wq1_t"], out["wo1_t"] = (t(a[x1 + n]) for n in ("Wk", "Wv", "Wq", "Wo"))
    out["wf_t"], out["vr_t"], out["cf_t"], out["bf"] = t(a[f1 + "W"]), t(a[f1 + "V_r"]), t(a[f1 + "C"]), a[f1 + "b"]
    out["before"] = np.triu(np.ones((S, S), np.float32), 1)
    out["iota"] = np.tile(np.arange(E, dtype=np.float32), (S, 1))
    out["lower"] = np.tile(np.tril(np.ones((E, E), np.float32), -1), (S, 1, 1))
    out["steps"] = np.tile(P * np.arange(NT_E, dtype=np.float32), (S, 1))
    out["tiles"] = np.tile(np.arange(NTILE, dtype=np.float32), (S, 1))
    out["qkv_bias"] = np.stack([a[x0 + n].reshape(C, P).T for n in ("bq", "bk", "bv")], 1)
    out["sb12"] = np.stack([a[f0 + n].reshape(SE * HM, P).T for n in ("sb1", "sb2")], 1)
    for n in ("bo", "g0", "beta0"):
        out[n] = a[x0 + n]
    for n in ("gate_w", "gate_b", "sw1", "sw2", "sw3", "sb3", "rw1", "rb1", "rw2", "rb2", "rw3", "rb3"):
        out[n] = a[f0 + n]
    return {k: np.ascontiguousarray(v) for k, v in out.items()}


def kernel(**inputs):
    import concourse.bacc as bacc
    import numpy as np
    from concourse.bass_utils import run_bass_kernel_spmd

    nc = bacc.Bacc("TRN2", target_bir_lowering=False, num_devices=1)
    arrays = {f"in_{name}": a for name, a in lay_out(inputs).items()}
    dram = {name[3:]: nc.dram_tensor(name, a.shape, mybir.dt.from_np(a.dtype), kind="ExternalInput").ap()
            for name, a in arrays.items()}
    outs = {"out": nc.dram_tensor("out", (B, S, D), F32, kind="ExternalOutput").ap()}
    build_program(nc, dram, outs)
    got = run_bass_kernel_spmd(nc, [arrays], core_ids=[0])
    return got.results[0]["out"]
```
